# Optimizing a Trainium2 kernel written in Bass

```python
import numpy as np
import jax
import jax.numpy as jnp

def _softmax(x, axis=-1):
    return jax.nn.softmax(x, axis=axis)

def _gelu(x):
    return jax.nn.gelu(x, approximate=True)

def _silu(x):
    return jax.nn.silu(x)

def _sigmoid(x):
    return jax.nn.sigmoid(x)

def _layernorm(x, axis=-1, eps=1e-05):
    m = jnp.mean(x, axis=axis, keepdims=True)
    v = jnp.var(x, axis=axis, keepdims=True)
    return (x - m) / jnp.sqrt(v + eps)

def _scatter_add(tgt, idx, src, axis=0):
    return tgt.at[idx].add(src)

def _segment_sum(src, seg, n):
    return jax.ops.segment_sum(src, seg, n)
kernel_name = 'mk_adaln_d1_jaxref_r8_e557ef'

def setup_inputs(seed: int=0):
    np.random.seed(seed)
    _w = jnp.asarray

    def _L0_attn_setup():
        import jax, jax.numpy as jnp
        import numpy as np
        EPS = 1e-06
        DECAY = 0.9
        THR = 0.5
        SBETA = 10.0
        KW = 4

        def _rms(x, w):
            return x * jax.lax.rsqrt(jnp.mean(x * x, axis=-1, keepdims=True) + EPS) * w
        B, T, D, H, dk, dv, r, dff = (2, 256, 128, 8, 64, 64, 64, 512)
        keys = iter(jax.random.split(jax.random.key(seed), 24))

        def g(shape, s=0.02):
            return jax.random.normal(next(keys), shape, jnp.float32) * s
        return {'x': jax.random.normal(next(keys), (B, T, D), jnp.float32), 'norm_in_w': jnp.ones((D,), jnp.float32), 'conv_w': g((D, 1, KW), 0.3), 'conv_b': jnp.zeros((D,), jnp.float32), 'Wq': g((D, H * dk)), 'Wk': g((D, H * dk)), 'Wv': g((D, H * dv)), 'Wo': g((H * dv, D)), 'Wspike': g((D, H * dk), 0.1), 'Wau': g((D, r)), 'bau': jnp.zeros((r,), jnp.float32), 'Wad': g((r, H * dk)), 'bad': jnp.zeros((H * dk,), jnp.float32), 'alpha_spike': jnp.zeros((1, H, dk), jnp.float32), 'Wbeta': g((D, H)), 'bbeta': jnp.zeros((H,), jnp.float32), 'beta_spike': jnp.zeros((1, H, dk), jnp.float32), 'head_norm_w': jnp.ones((H, dv), jnp.float32), 'Wu1': g((D, r)), 'bu1': jnp.zeros((r,), jnp.float32), 'Wu2': g((r, D)), 'bu2': jnp.zeros((D,), jnp.float32), 'ff_norm_w': jnp.ones((D,), jnp.float32), 'Wff1': g((D, dff)), 'Wff3': g((D, dff)), 'Wff2': g((dff, D))}
    _L0_attn_in = _L0_attn_setup()

    def _L0_ffn_setup():
        import jax, jax.numpy as jnp
        import numpy as np
        DIM = 128
        DEPTH = 6
        HEADS = 16
        DIM_HEAD = 64
        WINDOW = 32
        INNER = HEADS * DIM_HEAD
        DIM_INNER = int(DIM * 4 * 2 / 3)
        QK_SCALE = 8.0

        def shift_tokens(t):
            a, s = jnp.split(t, 2, -1)
            s = jnp.pad(s, ((0, 0), (1, 0), (0, 0)))[:, :-1]
            return jnp.concatenate([a, s], -1)

        def l2norm(t):
            return t / jnp.maximum(jnp.linalg.norm(t, axis=-1, keepdims=True), 1e-12)

        def rotate_half(x):
            x1, x2 = jnp.split(x, 2, -1)
            return jnp.concatenate([-x2, x1], -1)

        def rotary_tables(n):
            half = jnp.arange(0, DIM_HEAD, 2, dtype=jnp.float32)
            inv_freq = 1.0 / 10000.0 ** (half / DIM_HEAD)
            t = jnp.arange(n, dtype=jnp.float32)
            freqs = t[:, None] * inv_freq[None, :]
            freqs = jnp.concatenate([freqs, freqs], -1)
            base_scale = (half + 0.4 * DIM_HEAD) / (1.4 * DIM_HEAD)
            power = (t - n // 2) / (WINDOW // 2)
            scale = base_scale[None, :] ** power[:, None]
            scale = jnp.concatenate([scale, scale], -1)
            return (freqs, scale)

        def local_attention(q, k, v):
            b, h, n, d = q.shape
            w = WINDOW
            nw = n // w
            bq = q.reshape(b, h, nw, w, d)
            bk = k.reshape(b, h, nw, w, d)
            bv = v.reshape(b, h, nw, w, d)

            def look(t):
                p = jnp.pad(t, ((0, 0), (0, 0), (1, 0), (0, 0), (0, 0)))
                return jnp.concatenate([p[:, :, :nw], p[:, :, 1:]], axis=3)
            bk2, bv2 = (look(bk), look(bv))
            seq = jnp.arange(n).reshape(nw, w)
            seq_p = jnp.pad(seq, ((1, 0), (0, 0)), constant_values=-1)
            jt = jnp.concatenate([seq_p[:nw], seq_p[1:]], axis=1)
            it = seq[:, :, None]
            jb = jt[:, None, :]
            mask = (it < jb) | (it > jb + w) | (jb == -1)
            sim = jnp.einsum('bhwie,bhwje->bhwij', bq, bk2) * QK_SCALE
            sim = jnp.where(mask, -jnp.finfo(sim.dtype).max, sim)
            attn = jax.nn.softmax(sim, -1)
            out = jnp.einsum('bhwij,bhwje->bhwie', attn, bv2)
            return out.reshape(b, h, n, d)

        def attn_layer(x, Wqkv, qs, ksc, Wo):
            b, n, _ = x.shape
            qkv = x @ Wqkv
            q, k, v = jnp.split(qkv, 3, -1)
            sh = lambda t: t.reshape(b, n, HEADS, DIM_HEAD).transpose(0, 2, 1, 3)
            q, k, v = (sh(q), sh(k), sh(v))
            q = l2norm(q) * qs
            k = l2norm(k) * ksc
            freqs, scale = rotary_tables(n)
            cos, sin = (jnp.cos(freqs), jnp.sin(freqs))
            q = q * cos * scale + rotate_half(q) * sin * scale
            inv = 1.0 / scale
            k = k * cos * inv + rotate_half(k) * sin * inv
            out = local_attention(q, k, v)
            out = out.transpose(0, 2, 1, 3).reshape(b, n, INNER)
            return out @ Wo

        def ffn_layer(x, g, bln, W1, b1, W2, b2):
            mu = x.mean(-1, keepdims=True)
            var = ((x - mu) ** 2).mean(-1, keepdims=True)
            xn = (x - mu) / jnp.sqrt(var + 1e-05) * g + bln
            hg = xn @ W1 + b1
            a, gate = jnp.split(hg, 2, -1)
            return a * jax.nn.gelu(gate, approximate=False) @ W2 + b2
        key = jax.random.key(seed)
        ks = jax.random.split(key, 8)
        B, N = (2, 256)
        init = lambda k, shape: jax.random.normal(k, shape, jnp.float32) * 0.02
        return {'x': jax.random.normal(ks[0], (B, N, DIM), jnp.float32), 'Wqkv': init(ks[1], (DEPTH, DIM, 3 * INNER)), 'q_scale': jnp.ones((DEPTH, DIM_HEAD), jnp.float32), 'k_scale': jnp.ones((DEPTH, DIM_HEAD), jnp.float32), 'Wo': init(ks[2], (DEPTH, INNER, DIM)), 'ln_g': jnp.ones((DEPTH, DIM), jnp.float32), 'ln_b': jnp.zeros((DEPTH, DIM), jnp.float32), 'W1': init(ks[3], (DEPTH, DIM, 2 * DIM_INNER)), 'b1': jnp.zeros((DEPTH, 2 * DIM_INNER), jnp.float32), 'W2': init(ks[4], (DEPTH, DIM_INNER, DIM)), 'b2': jnp.zeros((DEPTH, DIM), jnp.float32)}
    _L0_ffn_in = _L0_ffn_setup()
    _L0_c = _w((lambda *s: np.random.randn(*s).astype(np.float32) * 0.05)(2, 128))
    _L0_wmod = _w((lambda *s: np.random.randn(*s).astype(np.float32) * 0.05)(128, 6 * 128) * 128 ** (-0.5))
    _d = {'L0_attn_x': _L0_attn_in['x'], 'L0_attn_norm_in_w': _L0_attn_in['norm_in_w'], 'L0_attn_conv_w': _L0_attn_in['conv_w'], 'L0_attn_conv_b': _L0_attn_in['conv_b'], 'L0_attn_Wq': _L0_attn_in['Wq'], 'L0_attn_Wk': _L0_attn_in['Wk'], 'L0_attn_Wv': _L0_attn_in['Wv'], 'L0_attn_Wo': _L0_attn_in['Wo'], 'L0_attn_Wspike': _L0_attn_in['Wspike'], 'L0_attn_Wau': _L0_attn_in['Wau'], 'L0_attn_bau': _L0_attn_in['bau'], 'L0_attn_Wad': _L0_attn_in['Wad'], 'L0_attn_bad': _L0_attn_in['bad'], 'L0_attn_alpha_spike': _L0_attn_in['alpha_spike'], 'L0_attn_Wbeta': _L0_attn_in['Wbeta'], 'L0_attn_bbeta': _L0_attn_in['bbeta'], 'L0_attn_beta_spike': _L0_attn_in['beta_spike'], 'L0_attn_head_norm_w': _L0_attn_in['head_norm_w'], 'L0_attn_Wu1': _L0_attn_in['Wu1'], 'L0_attn_bu1': _L0_attn_in['bu1'], 'L0_attn_Wu2': _L0_attn_in['Wu2'], 'L0_attn_bu2': _L0_attn_in['bu2'], 'L0_attn_ff_norm_w': _L0_attn_in['ff_norm_w'], 'L0_attn_Wff1': _L0_attn_in['Wff1'], 'L0_attn_Wff3': _L0_attn_in['Wff3'], 'L0_attn_Wff2': _L0_attn_in['Wff2'], 'L0_ffn_Wqkv': _L0_ffn_in['Wqkv'], 'L0_ffn_q_scale': _L0_ffn_in['q_scale'], 'L0_ffn_k_scale': _L0_ffn_in['k_scale'], 'L0_ffn_Wo': _L0_ffn_in['Wo'], 'L0_ffn_ln_g': _L0_ffn_in['ln_g'], 'L0_ffn_ln_b': _L0_ffn_in['ln_b'], 'L0_ffn_W1': _L0_ffn_in['W1'], 'L0_ffn_b1': _L0_ffn_in['b1'], 'L0_ffn_W2': _L0_ffn_in['W2'], 'L0_ffn_b2': _L0_ffn_in['b2'], 'L0_c': _L0_c, 'L0_wmod': _L0_wmod}
    _x0 = _d['L0_attn_x']
    _d['L0_attn_x'] = jax.random.normal(jax.random.fold_in(jax.random.key(seed), 1), (2, 2048, 128), dtype=_x0.dtype)
    del _x0
    return _d

def reference(L0_attn_x, L0_attn_norm_in_w, L0_attn_conv_w, L0_attn_conv_b, L0_attn_Wq, L0_attn_Wk, L0_attn_Wv, L0_attn_Wo, L0_attn_Wspike, L0_attn_Wau, L0_attn_bau, L0_attn_Wad, L0_attn_bad, L0_attn_alpha_spike, L0_attn_Wbeta, L0_attn_bbeta, L0_attn_beta_spike, L0_attn_head_norm_w, L0_attn_Wu1, L0_attn_bu1, L0_attn_Wu2, L0_attn_bu2, L0_attn_ff_norm_w, L0_attn_Wff1, L0_attn_Wff3, L0_attn_Wff2, L0_ffn_Wqkv, L0_ffn_q_scale, L0_ffn_k_scale, L0_ffn_Wo, L0_ffn_ln_g, L0_ffn_ln_b, L0_ffn_W1, L0_ffn_b1, L0_ffn_W2, L0_ffn_b2, L0_c, L0_wmod):

    def _L0_attn_ref(x, norm_in_w, conv_w, conv_b, Wq, Wk, Wv, Wo, Wspike, Wau, bau, Wad, bad, alpha_spike, Wbeta, bbeta, beta_spike, head_norm_w, Wu1, bu1, Wu2, bu2, ff_norm_w, Wff1, Wff3, Wff2):
        import jax, jax.numpy as jnp
        import numpy as np
        EPS = 1e-06
        DECAY = 0.9
        THR = 0.5
        SBETA = 10.0
        KW = 4

        def _rms(x, w):
            return x * jax.lax.rsqrt(jnp.mean(x * x, axis=-1, keepdims=True) + EPS) * w
        B, T, D = x.shape
        H, dk = (alpha_spike.shape[1], alpha_spike.shape[2])
        dv = head_norm_w.shape[1]
        h = _rms(x, norm_in_w)
        hc = jnp.transpose(h, (0, 2, 1))
        conv = jax.lax.conv_general_dilated(hc, conv_w, window_strides=(1,), padding=[(KW - 1, 0)], dimension_numbers=('NCH', 'OIH', 'NCH'), feature_group_count=D)
        conv = conv + conv_b[None, :, None]
        h = jax.nn.silu(jnp.transpose(conv, (0, 2, 1)))

        def heads(z, d):
            return z.reshape(B, T, H, d)
        q = heads(h @ Wq, dk)
        k = heads(h @ Wk, dk)
        v = heads(h @ Wv, dv)
        q = q / (jnp.linalg.norm(q, axis=-1, keepdims=True) + 1e-06)
        k = k / (jnp.linalg.norm(k, axis=-1, keepdims=True) + 1e-06)
        drive = heads(h @ Wspike, dk)
        alpha_base = heads(jax.nn.silu(h @ Wau + bau) @ Wad + bad, dk)
        beta_base = h @ Wbeta + bbeta
        asp = alpha_spike[0]
        bsp = beta_spike[0]

        def step(carry, ins):
            s, mem = carry
            qt, kt, vt, dt, at, bt = ins
            mem = DECAY * mem + dt
            sg = jax.nn.sigmoid(SBETA * (mem - THR))
            hard = (mem > THR).astype(mem.dtype)
            spike = sg + jax.lax.stop_gradient(hard - sg)
            mem = mem - spike * THR
            alpha = jax.nn.sigmoid(at + asp * spike)
            beta = jax.nn.sigmoid(bt[..., None] + jnp.sum(spike * bsp, -1, keepdims=True))
            active = (jnp.sum(jnp.abs(spike), -1, keepdims=True) > 0).astype(qt.dtype)
            alpha = jnp.where(active > 0, alpha, jnp.ones_like(alpha))
            beta = beta * active
            s = s * alpha[..., None]
            pred = jnp.einsum('bhk,bhkv->bhv', kt, s)
            s = s + (beta * kt)[..., None] * (vt - pred)[:, :, None, :]
            out = jnp.einsum('bhk,bhkv->bhv', qt, s)
            return ((s, mem), out)
        s0 = jnp.zeros((B, H, dk, dv), x.dtype)
        m0 = jnp.zeros((B, H, dk), x.dtype)
        xs = (jnp.moveaxis(q, 1, 0), jnp.moveaxis(k, 1, 0), jnp.moveaxis(v, 1, 0), jnp.moveaxis(drive, 1, 0), jnp.moveaxis(alpha_base, 1, 0), jnp.moveaxis(beta_base, 1, 0))
        _, y = jax.lax.scan(step, (s0, m0), xs)
        y = jnp.moveaxis(y, 0, 1)
        y = y * jax.lax.rsqrt(jnp.mean(y * y, axis=-1, keepdims=True) + EPS) * head_norm_w
        y = y.reshape(B, T, H * dv)
        gate = jax.nn.sigmoid(jax.nn.silu(x @ Wu1 + bu1) @ Wu2 + bu2)
        y = x + y @ Wo * gate
        z = _rms(y, ff_norm_w)
        y = y + jax.nn.silu(z @ Wff1) * (z @ Wff3) @ Wff2
        return y

    def _L0_ffn_ref(x, Wqkv, q_scale, k_scale, Wo, ln_g, ln_b, W1, b1, W2, b2):
        import jax, jax.numpy as jnp
        import numpy as np
        DIM = 128
        DEPTH = 6
        HEADS = 16
        DIM_HEAD = 64
        WINDOW = 32
        INNER = HEADS * DIM_HEAD
        DIM_INNER = int(DIM * 4 * 2 / 3)
        QK_SCALE = 8.0

        def shift_tokens(t):
            a, s = jnp.split(t, 2, -1)
            s = jnp.pad(s, ((0, 0), (1, 0), (0, 0)))[:, :-1]
            return jnp.concatenate([a, s], -1)

        def l2norm(t):
            return t / jnp.maximum(jnp.linalg.norm(t, axis=-1, keepdims=True), 1e-12)

        def rotate_half(x):
            x1, x2 = jnp.split(x, 2, -1)
            return jnp.concatenate([-x2, x1], -1)

        def rotary_tables(n):
            half = jnp.arange(0, DIM_HEAD, 2, dtype=jnp.float32)
            inv_freq = 1.0 / 10000.0 ** (half / DIM_HEAD)
            t = jnp.arange(n, dtype=jnp.float32)
            freqs = t[:, None] * inv_freq[None, :]
            freqs = jnp.concatenate([freqs, freqs], -1)
            base_scale = (half + 0.4 * DIM_HEAD) / (1.4 * DIM_HEAD)
            power = (t - n // 2) / (WINDOW // 2)
            scale = base_scale[None, :] ** power[:, None]
            scale = jnp.concatenate([scale, scale], -1)
            return (freqs, scale)

        def local_attention(q, k, v):
            b, h, n, d = q.shape
            w = WINDOW
            nw = n // w
            bq = q.reshape(b, h, nw, w, d)
            bk = k.reshape(b, h, nw, w, d)
            bv = v.reshape(b, h, nw, w, d)

            def look(t):
                p = jnp.pad(t, ((0, 0), (0, 0), (1, 0), (0, 0), (0, 0)))
                return jnp.concatenate([p[:, :, :nw], p[:, :, 1:]], axis=3)
            bk2, bv2 = (look(bk), look(bv))
            seq = jnp.arange(n).reshape(nw, w)
            seq_p = jnp.pad(seq, ((1, 0), (0, 0)), constant_values=-1)
            jt = jnp.concatenate([seq_p[:nw], seq_p[1:]], axis=1)
            it = seq[:, :, None]
            jb = jt[:, None, :]
            mask = (it < jb) | (it > jb + w) | (jb == -1)
            sim = jnp.einsum('bhwie,bhwje->bhwij', bq, bk2) * QK_SCALE
            sim = jnp.where(mask, -jnp.finfo(sim.dtype).max, sim)
            attn = jax.nn.softmax(sim, -1)
            out = jnp.einsum('bhwij,bhwje->bhwie', attn, bv2)
            return out.reshape(b, h, n, d)

        def attn_layer(x, Wqkv, qs, ksc, Wo):
            b, n, _ = x.shape
            qkv = x @ Wqkv
            q, k, v = jnp.split(qkv, 3, -1)
            sh = lambda t: t.reshape(b, n, HEADS, DIM_HEAD).transpose(0, 2, 1, 3)
            q, k, v = (sh(q), sh(k), sh(v))
            q = l2norm(q) * qs
            k = l2norm(k) * ksc
            freqs, scale = rotary_tables(n)
            cos, sin = (jnp.cos(freqs), jnp.sin(freqs))
            q = q * cos * scale + rotate_half(q) * sin * scale
            inv = 1.0 / scale
            k = k * cos * inv + rotate_half(k) * sin * inv
            out = local_attention(q, k, v)
            out = out.transpose(0, 2, 1, 3).reshape(b, n, INNER)
            return out @ Wo

        def ffn_layer(x, g, bln, W1, b1, W2, b2):
            mu = x.mean(-1, keepdims=True)
            var = ((x - mu) ** 2).mean(-1, keepdims=True)
            xn = (x - mu) / jnp.sqrt(var + 1e-05) * g + bln
            hg = xn @ W1 + b1
            a, gate = jnp.split(hg, 2, -1)
            return a * jax.nn.gelu(gate, approximate=False) @ W2 + b2
        for i in range(DEPTH):
            x = attn_layer(shift_tokens(x), Wqkv[i], q_scale[i], k_scale[i], Wo[i]) + x
            x = ffn_layer(shift_tokens(x), ln_g[i], ln_b[i], W1[i], b1[i], W2[i], b2[i]) + x
        return x
    x = L0_attn_x
    mod = (_silu(L0_c) @ L0_wmod).reshape(L0_c.shape[0], 6, 1, -1)
    sa, ca, ga, sb, cb, gb = (mod[:, 0], mod[:, 1], mod[:, 2], mod[:, 3], mod[:, 4], mod[:, 5])
    ga = (2 * (ga >= 0) - 1) * jnp.maximum(jnp.abs(ga), 0.25)
    gb = (2 * (gb >= 0) - 1) * jnp.maximum(jnp.abs(gb), 0.25)
    h = _layernorm(x, axis=-1) * (1 + ca) + sa
    x = x + ga * _L0_attn_ref(h, L0_attn_norm_in_w, L0_attn_conv_w, L0_attn_conv_b, L0_attn_Wq, L0_attn_Wk, L0_attn_Wv, L0_attn_Wo, L0_attn_Wspike, L0_attn_Wau, L0_attn_bau, L0_attn_Wad, L0_attn_bad, L0_attn_alpha_spike, L0_attn_Wbeta, L0_attn_bbeta, L0_attn_beta_spike, L0_attn_head_norm_w, L0_attn_Wu1, L0_attn_bu1, L0_attn_Wu2, L0_attn_bu2, L0_attn_ff_norm_w, L0_attn_Wff1, L0_attn_Wff3, L0_attn_Wff2)
    h = _layernorm(x, axis=-1) * (1 + cb) + sb
    x = x + gb * _L0_ffn_ref(h, L0_ffn_Wqkv, L0_ffn_q_scale, L0_ffn_k_scale, L0_ffn_Wo, L0_ffn_ln_g, L0_ffn_ln_b, L0_ffn_W1, L0_ffn_b1, L0_ffn_W2, L0_ffn_b2)
    return x

_drawn_inputs = setup_inputs


def setup_inputs(seed=0):
    import zlib

    import numpy as np

    out = dict(_drawn_inputs(seed))
    spreads = {'L0_attn_norm_in_w': (1.0, 0.6),
     'L0_attn_conv_b': (0.0, 0.432),
     'L0_attn_bau': (0.0, 0.8),
     'L0_attn_bad': (0.0, 0.8),
     'L0_attn_alpha_spike': (0.0, 0.8),
     'L0_attn_bbeta': (0.0, 0.8),
     'L0_attn_beta_spike': (0.0, 0.8),
     'L0_attn_head_norm_w': (1.0, 0.6),
     'L0_attn_bu1': (0.0, 0.8),
     'L0_attn_bu2': (0.0, 0.8),
     'L0_attn_ff_norm_w': (1.0, 0.6),
     'L0_ffn_q_scale': (1.0, 0.6),
     'L0_ffn_k_scale': (1.0, 0.6),
     'L0_ffn_ln_g': (1.0, 0.6),
     'L0_ffn_ln_b': (0.0, 0.8),
     'L0_ffn_b1': (0.0, 0.8),
     'L0_ffn_b2': (0.0, 0.715)}
    factors = {'L0_attn_Wspike': 8.0,
     'L0_attn_Wau': 8.0,
     'L0_attn_Wad': 8.0,
     'L0_attn_Wbeta': 8.0,
     'L0_attn_Wu1': 8.0,
     'L0_attn_Wu2': 8.0,
     'L0_attn_Wff1': 8.0,
     'L0_attn_Wff3': 8.0,
     'L0_attn_Wff2': 8.0,
     'L0_ffn_W1': 7.482,
     'L0_ffn_W2': 7.343}
    for name, (base, spread) in spreads.items():
        noise = np.random.default_rng([zlib.crc32(name.encode()), seed]).standard_normal(out[name].shape)
        drawn = base * np.exp(spread * noise) if base else spread * noise
        out[name] = jnp.asarray(drawn.astype(out[name].dtype))
    for name, factor in factors.items():
        out[name] = (out[name] * factor).astype(out[name].dtype)
    return out
```

```python
from contextlib import ExitStack

import concourse.bass as bass
import numpy as np
from concourse import mybir

F32 = mybir.dt.float32
U32 = mybir.dt.uint32
ALU = mybir.AluOpType
ACT = mybir.ActivationFunctionType
AX_X = mybir.AxisListType.X
LN_EXP = "natural_log_exp_and_others"

P = 128
D = 128
H = 8
DK = 64
C = 8
G = 64
NC = G // C
HEADS = 16
DH = 64
PAIRS = HEADS // 2
WIN = 32
HALO = WIN
XPAD = WIN + 1
TILE = 128
DECAY, THR = 0.9, 0.5
SIG_MIN = -43.0
LOG_DECAY_MAX = 20.7
NEG = -1e30
TINY = 1e-19


def shape_constants(T):
    p = np.arange(P)
    ident = np.eye(P, dtype=np.float32)
    ones_block = (p[:, None] // DK == p[None, :] // DK).astype(np.float32)
    r = p % 64
    col = np.arange(64)
    same = (r[:, None] // C) == (col[None, :] // C)
    rows_first = same & (r[:, None] % C < col[None, :] % C)
    rows_last = same & (r[:, None] % C > col[None, :] % C)
    rows_to = same & (r[:, None] % C <= col[None, :] % C)
    ident64 = (r[:, None] == col[None, :])
    head_of_row = (r[:, None] // C) == np.arange(H)[None, :]
    small = np.concatenate([ident, ones_block, rows_first, rows_last, rows_to, ident64, head_of_row],
                           axis=1).astype(np.float32)
    half = np.arange(0, DH, 2, dtype=np.float32)
    inv_freq = (np.float32(1.0) / np.float32(10000.0) ** (half / np.float32(DH))).astype(np.float32)
    t = np.arange(T, dtype=np.float32)
    freqs = t[:, None] * inv_freq[None, :]
    freqs = np.concatenate([freqs, freqs], -1).astype(np.float32)
    base = (half.astype(np.float64) + 0.4 * DH) / (1.4 * DH)
    base = np.concatenate([base, base])
    power = ((np.arange(T) % TILE) - TILE // 2) / (WIN // 2)
    scale = base[None, :] ** power[:, None]
    sign = np.where(np.arange(DH) < DH // 2, -1.0, 1.0)
    cos, sin = np.cos(freqs), np.sin(freqs)
    tabs = np.stack([cos * scale, sin * scale * sign, cos / scale, sin / scale * sign], axis=1)
    tabs = tabs.reshape(T // TILE, TILE, 4 * DH).transpose(1, 0, 2)
    tabs = np.concatenate([tabs, tabs], axis=1).astype(np.float32)
    i = np.arange(TILE) % WIN
    j = np.arange(WIN)
    m = np.concatenate([np.where(j[None, :] >= i[:, None], 0.0, NEG),
                        np.where(j[None, :] <= i[:, None], 0.0, NEG)], axis=1)
    first = m.copy()
    first[:WIN, :WIN] = NEG
    n = T // TILE
    masks = np.stack([first if k % n == 0 else m for k in range(2 * n)], axis=1).astype(np.float32)
    keep = np.stack([np.full(P, 0.0 if k % n == 0 else 1.0) for k in range(2 * n)], axis=1)
    halo = (base ** (TILE // (WIN // 2)))[p % DH][:, None]
    cols = np.concatenate([keep, halo], axis=1).astype(np.float32)
    return {"small": small, "tabs": np.ascontiguousarray(tabs), "masks": np.ascontiguousarray(masks),
            "cols": np.ascontiguousarray(cols)}


class Shared:
    pass


class Link:

    def __init__(self, eng, sem):
        self.eng, self.sem, self.n = eng, sem, 0

    def __call__(self, ins):
        self.n += 1
        ins.then_inc(self.sem, 1)
        self.eng.wait_ge(self.sem, self.n)

    def restart(self):
        self.eng.sem_clear(self.sem)
        self.n = 0



def sbuf(nc, scope, name, shape, dt=F32):
    return scope.enter_context(nc.sbuf_tensor(name, shape, dt))


def signals(nc, scope, prefix, names):
    return {n: scope.enter_context(nc.semaphore(f"{prefix}_{n}")) for n in names.split()}


def adaln_block(nc, a, const, out):
    T = a["L0_attn_x"].shape[2]
    BL = min(512, T)
    with ExitStack() as top:
        s = Shared()
        s.T, s.BL, s.NB = T, BL, T // BL
        s.a, s.const = a, const
        s.ps = top.enter_context(nc.psum_tensor("ps", [P, 8, 512], F32))
        s.x = sbuf(nc, top, "x_resid", [P, 2, T])
        s.small = sbuf(nc, top, "small_consts", [P, 2 * P + 4 * 64 + H])
        s.ident, s.ones_block = s.small[:, 0:P], s.small[:, P:2 * P]
        s.rows_first, s.rows_last, s.rows_to, s.ident64 = (
            s.small[:, 2 * P + 64 * k:2 * P + 64 * k + 64] for k in range(4))
        s.head_mask = s.small[:, 2 * P + 256:2 * P + 256 + H]
        s.ones = sbuf(nc, top, "ones", [P, P])
        s.mod = sbuf(nc, top, "mod", [P, 6, 2])
        s.xa = sbuf(nc, top, "xa", [P, XPAD + 2 * T])
        modulation(nc, s)
        with ExitStack() as attn:
            s.h = sbuf(nc, attn, "attn_in", [P, 2, T])
            s.y = sbuf(nc, attn, "recurrent_out", [P, 2, T])
            with ExitStack() as conv:
                s.conv = sbuf(nc, conv, "conv_out", [P, 2, T])
                norm_and_conv(nc, s)
                recurrence(nc, s)
            gate_and_ff(nc, s)
        windowed_layers(nc, s, out)


SH_A, SC_A, GATE_A, SH_B, SC_B, GATE_B = range(6)


def modulation(nc, s):
    a, mod = s.a, s.mod
    with ExitStack() as c:
        cT = sbuf(nc, c, "c_t", [P, 2])
        cs = sbuf(nc, c, "c_silu", [P, 2])
        g1 = sbuf(nc, c, "gate_sign", [P, 2])
        g2 = sbuf(nc, c, "gate_size", [P, 2])
        wmod = sbuf(nc, c, "wmod", [P, 6 * P])
        q = signals(nc, c, "mod", "loaded sigmoid silu product dve act")
        with nc.Block() as block:
            @block.sync
            def _(sp):
                sp.dma_start(cT[:], a["L0_c"]).then_inc(q["loaded"], 16)
                sp.dma_start(wmod[:], a["L0_wmod"]).then_inc(q["loaded"], 16)
                sp.dma_start(s.small[:], s.const["small"]).then_inc(q["loaded"], 16)

            @block.scalar
            def _(act):
                act.preload_act_table_set(LN_EXP)
                own = Link(act, q["act"])
                act.wait_ge(q["loaded"], 48)
                own(act.activation(g1[:], cT[:], ACT.Exp, scale=-1.0))
                own(act.activation(g1[:], g1[:], ACT.Ln, bias=1.0))
                act.activation(g1[:], g1[:], ACT.Exp, scale=-1.0).then_inc(q["sigmoid"], 1)

            @block.tensor
            def _(pe):
                pe.wait_ge(q["silu"], 1)
                for k in range(6):
                    ins = pe.matmul(s.ps[:, 0, 2 * k:2 * k + 2], wmod[:, P * k:P * k + P], cs[:],
                                    start=True, stop=True)
                ins.then_inc(q["product"], 1)

            @block.vector
            def _(dve):
                own = Link(dve, q["dve"])
                own(dve.memset(s.ones[:], 1.0))
                dve.wait_ge(q["sigmoid"], 1)
                dve.tensor_tensor(cs[:], cT[:], g1[:], ALU.mult).then_inc(q["silu"], 1)
                dve.wait_ge(q["product"], 1)
                own(dve.tensor_copy(mod[:].rearrange("p k b -> p (k b)"), s.ps[:, 0, 0:12]))
                for k in (SC_A, SC_B):
                    own(dve.tensor_scalar(mod[:, k, :], mod[:, k, :], 1.0, None, ALU.add))
                for k in (GATE_A, GATE_B):
                    own(dve.tensor_scalar(g1[:], mod[:, k, :], 0.0, 2.0, ALU.is_ge, ALU.mult))
                    own(dve.tensor_scalar(g2[:], mod[:, k, :], -1.0, 0.25, ALU.mult, ALU.max))
                    own(dve.tensor_tensor(g2[:], g2[:], mod[:, k, :], ALU.max))
                    own(dve.scalar_tensor_tensor(out=mod[:, k, :], in0=g1[:], scalar=-1.0, in1=g2[:],
                                                 op0=ALU.add, op1=ALU.mult))


def halves(s, bank0=None):
    return [s.ps[:, 4 * b:4 * b + s.NB, 0:s.BL] for b in range(2)]


def norm_and_conv(nc, s):
    a, T, NB, BL, ps, mod = s.a, s.T, s.NB, s.BL, s.ps, s.mod
    with ExitStack() as c:
        w1 = sbuf(nc, c, "nc_values", [P, 2, T])
        w2 = sbuf(nc, c, "nc_factors", [P, 2, T])
        rp = sbuf(nc, c, "nc_rms", [P, 2, T + 3])
        vecs = sbuf(nc, c, "nc_vectors", [P, 6])
        q = signals(nc, c, "nc", "x0_in x1_in vecs_in sums centered squares h squares_h rstd "
                                 "conv sigmoid dve act")
        x_in = [q["x0_in"], q["x1_in"]]
        banks = halves(s)
        blk = lambda t, b: t[:, b, :].rearrange("p (n l) -> p n l", l=BL)
        with nc.Block() as block:
            @block.sync
            def _(sp):
                for b in range(2):
                    sp.dma_start(s.x[:, b, :], a["L0_attn_x"][:, b, :]).then_inc(x_in[b], 16)
                sp.dma_start(vecs[:, 0:1], a["L0_attn_norm_in_w"].unsqueeze(1)).then_inc(q["vecs_in"], 16)
                sp.dma_start(vecs[:, 1:2], a["L0_attn_conv_b"].unsqueeze(1)).then_inc(q["vecs_in"], 16)
                sp.dma_start(vecs[:, 2:6], a["L0_attn_conv_w"].rearrange("c o k -> c (o k)"))\
                  .then_inc(q["vecs_in"], 16)

            @block.tensor
            def _(pe):
                for ready, src in ((None, s.x), (q["squares"], w2), (q["squares_h"], w2)):
                    for b in range(2):
                        pe.wait_ge(ready or x_in[b], b + 1 if ready else 16)
                        for n in range(NB):
                            ins = pe.matmul(ps[:, 4 * b + n, 0:BL], s.ones[:], src[:, b, BL * n:BL * n + BL],
                                            start=True, stop=True)
                        ins.then_inc(q["sums"], 1)

            @block.scalar
            def _(act):
                own = Link(act, q["act"])
                for b in range(2):
                    act.wait_ge(q["centered"], b + 1)
                    act.activation(w2[:, b, :], w1[:, b, :], ACT.Square).then_inc(q["squares"], 1)
                for b in range(2):
                    act.wait_ge(q["sums"], b + 3)
                    own(act.activation(blk(w2, b), banks[b], ACT.Ln, scale=1.0 / D, bias=1e-5))
                    act.activation(w2[:, b, :], w2[:, b, :], ACT.Exp, scale=-0.5).then_inc(q["rstd"], 1)
                for b in range(2):
                    act.wait_ge(q["h"], b + 1)
                    act.activation(w2[:, b, :], s.h[:, b, :], ACT.Square).then_inc(q["squares_h"], 1)
                for b in range(2):
                    act.wait_ge(q["sums"], b + 5)
                    own(act.activation(blk(w2, b), banks[b], ACT.Ln, scale=1.0 / D, bias=1e-6))
                    act.activation(w2[:, b, :], w2[:, b, :], ACT.Exp, scale=-0.5).then_inc(q["rstd"], 1)
                for b in range(2):
                    act.wait_ge(q["conv"], b + 1)
                    own(act.activation(w2[:, b, :], w2[:, b, :], ACT.Exp, scale=-1.0))
                    own(act.activation(w2[:, b, :], w2[:, b, :], ACT.Ln, bias=1.0))
                    act.activation(w2[:, b, :], w2[:, b, :], ACT.Exp, scale=-1.0).then_inc(q["sigmoid"], 1)

            @block.vector
            def _(dve):
                own = Link(dve, q["dve"])
                own(dve.memset(rp[:, :, 0:3], 0.0))
                for b in range(2):
                    dve.wait_ge(q["sums"], b + 1)
                    dve.scalar_tensor_tensor(out=blk(w1, b), in0=banks[b], scalar=-1.0 / D, in1=blk(s.x, b),
                                             op0=ALU.mult, op1=ALU.add).then_inc(q["centered"], 1)
                for b in range(2):
                    dve.wait_ge(q["rstd"], b + 1)
                    dve.wait_ge(q["centered"], b + 1)
                    own(dve.tensor_tensor(w1[:, b, :], w1[:, b, :], w2[:, b, :], ALU.mult))
                    dve.tensor_scalar(s.h[:, b, :], w1[:, b, :], mod[:, SC_A, b:b + 1], mod[:, SH_A, b:b + 1],
                                      ALU.mult, ALU.add).then_inc(q["h"], 1)
                dve.wait_ge(q["vecs_in"], 48)
                for b in range(2):
                    dve.wait_ge(q["rstd"], b + 3)
                    dve.wait_ge(q["h"], b + 1)
                    own(dve.scalar_tensor_tensor(out=rp[:, b, 3:3 + T], in0=s.h[:, b, :], scalar=vecs[:, 0:1],
                                                 in1=w2[:, b, :], op0=ALU.mult, op1=ALU.mult))
                    own(dve.tensor_scalar(w1[:, b, :], rp[:, b, 0:T], vecs[:, 2:3], vecs[:, 1:2],
                                          ALU.mult, ALU.add))
                    for k in range(1, 4):
                        own(dve.scalar_tensor_tensor(out=w1[:, b, :], in0=rp[:, b, k:k + T],
                                                     scalar=vecs[:, 2 + k:3 + k], in1=w1[:, b, :],
                                                     op0=ALU.mult, op1=ALU.add))
                    dve.tensor_scalar(w2[:, b, :], w1[:, b, :], SIG_MIN, None, ALU.max).then_inc(q["conv"], 1)
                for b in range(2):
                    dve.wait_ge(q["sigmoid"], b + 1)
                    own(dve.tensor_tensor(s.conv[:, b, :], w1[:, b, :], w2[:, b, :], ALU.mult))


def recurrence(nc, s):
    a, T, ps = s.a, s.T, s.ps
    R = a["L0_attn_Wau"].shape[1]
    NG = T // G
    assert NC == 8 and H == 8 and C == 8 and G == 64 and R == 64
    with ExitStack() as c:
        def sb(name, shape):
            return sbuf(nc, c, name, shape)

        def full(name):
            return sb(name, [P, NC, H, C])

        w4 = sb("rc_w4", [P, 4, H * DK])
        wau = sb("rc_wau", [P, R])
        wad = sb("rc_wad", [R + 1, H * DK])
        wbeta = sb("rc_wbeta", [P, H])
        wbeta_rep = sb("rc_wbeta_rep", [P, H, DK])
        bsp = sb("rc_bsp", [P, H])
        bsp_rep = sb("rc_bsp_rep", [P, H, DK])
        asp = sb("rc_asp", [P, H])
        bbeta = sb("rc_bbeta", [P, H])
        norm_w = sb("rc_norm_w", [P, H])
        bau = sb("rc_bau", [R, 1])
        wo = sb("rc_wo", [P, H, D])
        xg = sb("rc_xg", [P, 2, G])
        sq = sb("rc_sq", [P, 2, 512])
        rn = sb("rc_rn", [P, 2, 512])
        qn, kn, dr, mp, spk, al, be, ex, ea, eb = (full(f"rc_{n}") for n in
                                                   "qn kn dr mp spk al be ex ea eb".split())
        au = sb("rc_au", [R, 2 * G])
        aus = sb("rc_aus", [R + 1, 2 * G])
        aux = sb("rc_aux", [R, 2 * G])
        neg_mem = sb("rc_neg_mem", [P, H])
        lg = sb("rc_lg", [P, NC * H])
        gm = sb("rc_gm", [P, NC * H])
        p8 = sb("rc_p8", [P, NC, H])
        qa, ka, kb, kab, kcb, kd, vb, t1 = (full(f"rc_{n}") for n in "qa ka kb kab kcb kd vb t1".split())
        wq = sb("rc_wq", [P, NC, H, 2, C])
        mt, mm, bt, imt, m2t, m2, m4, p1, tt, kcr, vbr, u0, ot = (
            sb(f"rc_{n}", [P, NC, 64]) for n in "mt mm bt imt m2t m2 m4 p1 tt kcr vbr u0 ot".split())
        kdx = sb("rc_kdx", [P, NC, P])
        S = sb("rc_state", [P, H, DK])
        sd = sb("rc_state_decayed", [P, H, DK])
        ut = sb("rc_ut", [P, 64])
        ur = sb("rc_ur", [P, 64])
        ux = sb("rc_ux", [P, H, DK])
        q = signals(nc, c, "rc", "w_in ready xg qkvd_done au_done squared sums nq recip au_ready au_sig aus_ready "
                    "spikes cnt_done alpha_mm beta_mm al_ready be_ready al_log be_sig ex_ready exps kqv_ready "
                    "m_mm m_ready m2_mm m2_ready m4_mm p1_ready m4_ready tt_mm tt_ready rows_mm rows_ready "
                    "w_mm u0_ready wq_ready xq_mm ut_ready ur_mm ur_ready ux_ready ds_mm bu_mm ot_ready s_ready "
                    "osq omean orms y_ready wo_mm y0_out y_out pe_turn dve_turn dve act")
        flat = lambda t: t[:].rearrange("p c h i -> p (c h i)")
        rows = lambda t: t[:].rearrange("p c h i -> p (c h) i")
        bank = lambda n: ps[:, n, :]
        bank_chi = lambda n: ps[:, n, :].rearrange("p (c h i) -> p c h i", c=NC, h=H)
        bank_ci = lambda n: ps[:, n, :].rearrange("p (c i) -> p c i", c=NC)
        per_head = lambda t: t[:].unsqueeze(1).unsqueeze(3).broadcast_to([P, NC, H, C])
        HALF = [slice(64 * b, 64 * b + 64) for b in range(2)]
        Q, K, V, DRV, AU, AL, SUM0, SUM1 = range(8)

        with nc.Block() as block:
            @block.sync
            def _(sp):
                for n, name in enumerate(("Wq", "Wk", "Wv", "Wspike")):
                    sp.dma_start(w4[:, n, :], a["L0_attn_" + name]).then_inc(q["w_in"], 16)
                sp.dma_start(wau[:], a["L0_attn_Wau"]).then_inc(q["w_in"], 16)
                sp.dma_start(wad[0:R, :], a["L0_attn_Wad"]).then_inc(q["w_in"], 16)
                sp.dma_start(wad[R:R + 1, :], a["L0_attn_bad"].unsqueeze(0)).then_inc(q["w_in"], 16)
                sp.dma_start(wbeta[:], a["L0_attn_Wbeta"]).then_inc(q["w_in"], 16)
                sp.dma_start(bbeta[:], a["L0_attn_bbeta"].unsqueeze(0).broadcast_to([P, H])).then_inc(q["w_in"], 16)
                sp.dma_start(bau[:], a["L0_attn_bau"].unsqueeze(1)).then_inc(q["w_in"], 16)
                for b in range(2):
                    sp.dma_start(bsp[HALF[b], :], a["L0_attn_beta_spike"][0])\
                      .then_inc(q["w_in"], 16)
                    sp.dma_start(asp[HALF[b], :], a["L0_attn_alpha_spike"][0])\
                      .then_inc(q["w_in"], 16)
                    sp.dma_start(norm_w[HALF[b], :], a["L0_attn_head_norm_w"])\
                      .then_inc(q["w_in"], 16)
                    sp.dma_start(wo[HALF[b], :, :], a["L0_attn_Wo"].rearrange("(h v) n -> v h n", v=DK))\
                      .then_inc(q["w_in"], 16)

            @block.gpsimd
            def _(pool):
                with pool.Fori(0, NG) as g:
                    pool.wait_ge(q["beta_mm"], g)
                    pool.tensor_copy(xg[:], s.conv[:, :, bass.ds(g * G, G)]).then_inc(q["xg"], 1)

            @block.tensor
            def _(pe):
                def hold():
                    pe.sem_inc(q["pe_turn"], 1)

                def both(bank_n, lhs, rhs, width=64):
                    for n in range(NC):
                        for b in range(2):
                            ins = pe.matmul(ps[HALF[b], bank_n, 64 * n:64 * n + width], lhs(n, b), rhs(n, b),
                                            start=True, stop=True)
                    return ins

                chunk = lambda t: (lambda n, b: t[HALF[b], n].rearrange("p h i -> p (h i)"))
                mat = lambda t: (lambda n, b: t[HALF[b], n, :])
                eye = lambda n, b: s.ident[HALF[b], HALF[b]]

                pe.wait_ge(q["w_in"], 18 * 16)
                pe.wait_ge(q["ready"], 1)
                with pe.Fori(0, NG) as g:
                    pe.wait_ge(q["xg"], g + 1)
                    pe.wait_ge(q["y_out"], g)
                    hold()
                    for n in range(4):
                        for h in range(H):
                            for b in range(2):
                                ins = pe.matmul(bank_chi(n)[HALF[b], :, h, :], w4[:, n, DK * h:DK * h + DK],
                                                xg[:, b, :], start=True, stop=True)
                        ins.then_inc(q["qkvd_done"], 1)
                    pe.matmul(ps[0:R, AU, 0:2 * G], wau[:], xg[:].rearrange("p b t -> p (b t)"),
                              start=True, stop=True).then_inc(q["au_done"], 1)
                    for n in range(2):
                        pe.wait_ge(q["squared"], 2 * g + n + 1)
                        pe.matmul(bank(SUM0 + n), s.ones_block, sq[:, n, :], start=True, stop=True)\
                          .then_inc(q["sums"], 1)
                    pe.wait_ge(q["aus_ready"], g + 1)
                    hold()
                    for h in range(H):
                        for b in range(2):
                            ins = pe.matmul(bank_chi(AL)[HALF[b], :, h, :], wad[:, DK * h:DK * h + DK],
                                            aus[:, G * b:G * b + G], start=True, stop=True)
                    ins.then_inc(q["alpha_mm"], 1)
                    pe.wait_ge(q["nq"], g + 1)
                    pe.wait_ge(q["spikes"], g + 1)
                    pe.matmul(bank(SUM0), s.ones_block, flat(spk), start=True, stop=True).then_inc(q["cnt_done"], 1)
                    for h in range(H):
                        for b in range(2):
                            o = bank_chi(DRV)[HALF[b], :, h, :]
                            pe.matmul(o, wbeta_rep[:, h, :], xg[:, b, :], start=True, stop=False,
                                      skip_group_check=True)
                            ins = pe.matmul(o, bsp_rep[HALF[b], h, :], spk[HALF[b], :, h, :],
                                            start=False, stop=True, skip_group_check=True)
                    ins.then_inc(q["beta_mm"], 1)
                    pe.wait_ge(q["kqv_ready"], g + 1)
                    hold()
                    both(Q, chunk(kb), chunk(kab))
                    both(K, chunk(kab), chunk(kb))
                    both(DRV, chunk(kb), chunk(qa)).then_inc(q["m_mm"], 1)
                    both(V, chunk(vb), eye)
                    both(AL, chunk(kcb), eye)
                    both(SUM1, chunk(kd), eye).then_inc(q["rows_mm"], 1)
                    pe.wait_ge(q["m_ready"], g + 1)
                    hold()
                    both(Q, mat(mm), mat(mt))
                    both(K, mat(mt), mat(mm)).then_inc(q["m2_mm"], 1)
                    pe.wait_ge(q["m2_ready"], g + 1)
                    hold()
                    both(DRV, mat(m2), mat(imt))
                    both(AU, mat(m2t), mat(m2)).then_inc(q["m4_mm"], 1)
                    pe.wait_ge(q["p1_ready"], g + 1)
                    pe.wait_ge(q["m4_ready"], g + 1)
                    hold()
                    both(Q, mat(m4), mat(p1)).then_inc(q["tt_mm"], 1)
                    pe.wait_ge(q["tt_ready"], g + 1)
                    pe.wait_ge(q["rows_ready"], g + 1)
                    hold()
                    both(SUM0, mat(kcr), mat(tt))
                    both(SUM1, mat(vbr), mat(tt)).then_inc(q["w_mm"], 1)
                    pe.wait_ge(q["wq_ready"], g + 1)
                    for n in range(NC):
                        xq = ps[:, 3 * (n % 2), 0:2 * 64].rearrange("p (h k i) -> p h k i", h=H, k=2)
                        pe.wait_ge(q["s_ready"], g * NC + n + 1)
                        if n >= 2:
                            pe.wait_ge(q["ot_ready"], g * NC + n - 1)
                        hold()
                        for h in range(H):
                            for b in range(2):
                                ins = pe.matmul(xq[HALF[b], h, :, :], S[HALF[b], h, :], wq[HALF[b], n, h, :, :],
                                                start=(h == 0), stop=False, skip_group_check=True)
                        ins.then_inc(q["xq_mm"], 1)
                        pe.wait_ge(q["ut_ready"], g * NC + n + 1)
                        hold()
                        for k in (K, AL):
                            for b in range(2):
                                ins = pe.matmul(ps[HALF[b], k, 0:64], ut[HALF[b], :], eye(n, b),
                                                start=True, stop=True)
                        ins.then_inc(q["ur_mm"], 1)
                        pe.wait_ge(q["ux_ready"], g * NC + n + 1)
                        pe.matmul(bank(V), kdx[:, n, :], ux[:].rearrange("p h v -> p (h v)"),
                                  start=True, stop=True).then_inc(q["ds_mm"], 1)
                        pe.wait_ge(q["ur_ready"], g * NC + n + 1)
                        hold()
                        for b in range(2):
                            ins = pe.matmul(xq[HALF[b], :, 1, :], ur[HALF[b], :], bt[HALF[b], n, :],
                                            start=False, stop=True, skip_group_check=True)
                        ins.then_inc(q["bu_mm"], 1)
                    pe.wait_ge(q["osq"], g + 1)
                    pe.matmul(bank(SUM0), s.ones_block, sq[:, 0, :], start=True, stop=True).then_inc(q["omean"], 1)
                    pe.wait_ge(q["y_ready"], g + 1)
                    hold()
                    for b in range(2):
                        for h in range(H):
                            ins = pe.matmul(ps[:, AL + 2 * b, 0:G], wo[HALF[b], h, :], t1[HALF[b], :, h, :],
                                            start=(h == 0), stop=(h == H - 1))
                    ins.then_inc(q["wo_mm"], 1)

            @block.scalar
            def _(act):
                def sigmoid_log(t):
                    own(act.activation(t, t, ACT.Exp, scale=-1.0))
                    return act.activation(t, t, ACT.Ln, bias=1.0)

                own = Link(act, q["act"])
                with act.Fori(0, NG) as g:
                    own.restart()
                    for n in range(2):
                        act.wait_ge(q["qkvd_done"], 4 * g + n + 1)
                        act.activation(sq[:, n, :], bank(n), ACT.Square).then_inc(q["squared"], 1)
                    act.wait_ge(q["nq"], g + 1)
                    own(act.activation(rn[:], rn[:], ACT.Ln))
                    own(act.activation(rn[:], rn[:], ACT.Exp, scale=0.5))
                    own(act.activation(rn[:], rn[:], ACT.Ln, bias=1e-6))
                    act.activation(rn[:], rn[:], ACT.Exp, scale=-1.0).then_inc(q["recip"], 1)
                    act.wait_ge(q["au_ready"], g + 1)
                    own(sigmoid_log(aux[:]))
                    act.activation(aux[:], aux[:], ACT.Exp, scale=-1.0).then_inc(q["au_sig"], 1)
                    act.wait_ge(q["al_ready"], g + 1)
                    sigmoid_log(flat(al)).then_inc(q["al_log"], 1)
                    act.wait_ge(q["be_ready"], g + 1)
                    own(sigmoid_log(flat(be)))
                    act.activation(flat(be), flat(be), ACT.Exp, scale=-1.0).then_inc(q["be_sig"], 1)
                    act.wait_ge(q["ex_ready"], g + 1)
                    own(act.activation(flat(ea), flat(ex), ACT.Exp, scale=-1.0))
                    own(act.activation(flat(eb), flat(ex), ACT.Exp))
                    own(act.activation(gm[:], lg[:], ACT.Exp))
                    act.activation(p8[:].rearrange("p c h -> p (c h)"), p8[:].rearrange("p c h -> p (c h)"),
                                   ACT.Exp).then_inc(q["exps"], 1)
                    act.wait_ge(q["rows_mm"], g + 1)
                    own(act.activation(vbr[:], bank_ci(V), ACT.Copy))
                    own(act.activation(kcr[:], bank_ci(AL), ACT.Copy))
                    own(act.activation(kdx[HALF[0], :, HALF[0]], bank_ci(SUM1)[HALF[0]], ACT.Copy))
                    act.activation(kdx[HALF[1], :, HALF[1]], bank_ci(SUM1)[HALF[1]], ACT.Copy)\
                       .then_inc(q["rows_ready"], 1)
                    act.wait_ge(q["m2_mm"], g + 1)
                    own(act.activation(m2t[:], bank_ci(Q), ACT.Copy))
                    act.activation(m2[:], bank_ci(K), ACT.Copy).then_inc(q["m2_ready"], 1)
                    act.wait_ge(q["m4_mm"], g + 1)
                    act.activation(m4[:], bank_ci(AU), ACT.Copy).then_inc(q["m4_ready"], 1)
                    act.wait_ge(q["w_mm"], g + 1)
                    own(act.activation(wq[:, :, :, 0, :].rearrange("p c h i -> p (c h) i"),
                                       bank(SUM0).rearrange("p (n i) -> p n i", i=C), ACT.Copy))
                    act.activation(u0[:], bank_ci(SUM1), ACT.Copy).then_inc(q["wq_ready"], 1)
                    for n in range(NC):
                        xq = ps[:, 3 * (n % 2), 0:2 * 64].rearrange("p (h k i) -> p h k i", h=H, k=2)
                        act.wait_ge(q["ur_mm"], g * NC + n + 1)
                        if n == 0:
                            act.wait_ge(q["bu_mm"], g * NC)
                        else:
                            act.wait_ge(q["bu_mm"], g * NC + n)
                        act.activation(ur[:], ps[:, AL, 0:64], ACT.Copy).then_inc(q["ur_ready"], 1)
                        act.wait_ge(q["bu_mm"], g * NC + n + 1)
                        act.activation(ot[:, n, :].rearrange("p (h i) -> p h i", h=H), xq[:, :, 1, :], ACT.Copy)\
                           .then_inc(q["ot_ready"], 1)
                    act.wait_ge(q["ot_ready"], g * NC + NC)
                    act.activation(sq[:, 0, :], ot[:].rearrange("p c i -> p (c i)"), ACT.Square).then_inc(q["osq"], 1)
                    act.wait_ge(q["omean"], g + 1)
                    own(act.activation(rn[:, 0, :], bank(SUM0), ACT.Ln, scale=1.0 / DK, bias=1e-6))
                    act.activation(rn[:, 0, :], rn[:, 0, :], ACT.Exp, scale=-0.5).then_inc(q["orms"], 1)
                    act.wait_ge(q["wo_mm"], g + 1)
                    act.activation(s.y[:, 0, bass.ds(g * G, G)], ps[:, AL, 0:G], ACT.Copy).then_inc(q["y0_out"], 1)
                    act.activation(s.y[:, 1, bass.ds(g * G, G)], ps[:, AL + 2, 0:G], ACT.Copy).then_inc(q["y_out"], 1)

            @block.vector
            def _(dve):
                own = Link(dve, q["dve"])
                own(dve.memset(neg_mem[:], 0.0))
                own(dve.memset(aus[:], 1.0))
                own(dve.memset(ex[:], 0.0))
                for t in (mt, mm, bt, kdx):
                    own(dve.memset(t[:], 0.0))
                dve.memset(S[:], 0.0).then_inc(q["s_ready"], 1)
                dve.wait_ge(q["w_in"], 18 * 16)
                own(dve.tensor_copy(wbeta_rep[:], wbeta[:].unsqueeze(2).broadcast_to([P, H, DK])))
                dve.tensor_copy(bsp_rep[:], bsp[:].unsqueeze(2).broadcast_to([P, H, DK])).then_inc(q["ready"], 1)
                dve.wait_ge(q["ready"], 1)
                dve.wait_ge(q["s_ready"], 1)
                exr, alr = rows(ex), rows(al)
                with dve.Fori(0, NG) as g:
                    own.restart()
                    dve.wait_ge(q["sums"], 2 * g + 2)
                    dve.tensor_scalar(rn[:].rearrange("p a n -> p (a n)"),
                                      ps[:, SUM0:SUM0 + 2, :].rearrange("p a n -> p (a n)"), TINY, None, ALU.max)\
                       .then_inc(q["nq"], 1)
                    dve.wait_ge(q["qkvd_done"], 4 * g + 4)
                    own(dve.tensor_scalar(flat(dr), bank(DRV), 1.0 / THR, None, ALU.mult))
                    dve.wait_ge(q["au_done"], g + 1)
                    own(dve.tensor_scalar(au[:], ps[0:R, AU, 0:2 * G], bau[:, 0:1], None, ALU.add))
                    dve.tensor_scalar(aux[:], au[:], SIG_MIN, None, ALU.max).then_inc(q["au_ready"], 1)
                    for n in range(NC):
                        for i in range(C):
                            own(dve.scalar_tensor_tensor(out=mp[:, n, :, i], in0=neg_mem[:], scalar=-DECAY,
                                                         in1=dr[:, n, :, i], op0=ALU.mult, op1=ALU.add))
                            own(dve.scalar_tensor_tensor(out=neg_mem[:], in0=mp[:, n, :, i], scalar=1.0,
                                                         in1=mp[:, n, :, i], op0=ALU.is_gt, op1=ALU.subtract))
                    dve.tensor_scalar(flat(spk), flat(mp), 1.0, None, ALU.is_gt).then_inc(q["spikes"], 1)
                    dve.wait_ge(q["au_sig"], g + 1)
                    dve.tensor_tensor(aus[0:R, :], au[:], aux[:], ALU.mult).then_inc(q["aus_ready"], 1)
                    dve.wait_ge(q["recip"], g + 1)
                    own(dve.tensor_tensor(flat(qn), bank(Q), rn[:, 0, :], ALU.mult))
                    own(dve.tensor_tensor(flat(kn), bank(K), rn[:, 1, :], ALU.mult))
                    dve.wait_ge(q["spikes"], g + 1)
                    own(dve.tensor_tensor(al[:], spk[:], per_head(asp), ALU.mult))
                    dve.wait_ge(q["alpha_mm"], g + 1)
                    own(dve.tensor_tensor(flat(al), flat(al), bank(AL), ALU.add))
                    dve.tensor_scalar(flat(al), flat(al), SIG_MIN, None, ALU.max).then_inc(q["al_ready"], 1)
                    dve.wait_ge(q["beta_mm"], g + 1)
                    own(dve.tensor_tensor(be[:], bank_chi(DRV), per_head(bbeta), ALU.add))
                    dve.tensor_scalar(flat(be), flat(be), SIG_MIN, None, ALU.max).then_inc(q["be_ready"], 1)
                    dve.wait_ge(q["cnt_done"], g + 1)
                    own(dve.tensor_scalar(flat(t1), bank(SUM0), 0.5, None, ALU.is_gt))
                    dve.wait_ge(q["al_log"], g + 1)
                    own(dve.scalar_tensor_tensor(out=flat(al), in0=flat(al), scalar=LOG_DECAY_MAX, in1=flat(t1),
                                                 op0=ALU.min, op1=ALU.mult))
                    own(dve.tensor_scalar(exr[:, :, 2], alr[:, :, 3], -1.0, None, ALU.mult))
                    for i in (1, 0):
                        own(dve.tensor_tensor(exr[:, :, i], exr[:, :, i + 1], alr[:, :, i + 1], ALU.subtract))
                    own(dve.tensor_tensor(lg[:], exr[:, :, 0], alr[:, :, 0], ALU.subtract))
                    own(dve.tensor_copy(exr[:, :, 4], alr[:, :, 4]))
                    for i in (5, 6, 7):
                        own(dve.tensor_tensor(exr[:, :, i], exr[:, :, i - 1], alr[:, :, i], ALU.add))
                    dve.tensor_tensor(p8[:].rearrange("p c h -> p (c h)"), lg[:], exr[:, :, 7], ALU.subtract)\
                       .then_inc(q["ex_ready"], 1)
                    dve.wait_ge(q["be_sig"], g + 1)
                    own(dve.tensor_tensor(flat(be), flat(be), flat(t1), ALU.mult))
                    dve.wait_ge(q["exps"], g + 1)
                    own(dve.tensor_tensor(flat(vb), bank(V), flat(be), ALU.mult))
                    own(dve.tensor_tensor(flat(qa), flat(qn), flat(ea), ALU.mult))
                    own(dve.tensor_tensor(flat(ka), flat(kn), flat(ea), ALU.mult))
                    own(dve.tensor_tensor(flat(kb), flat(kn), flat(eb), ALU.mult))
                    own(dve.scalar_tensor_tensor(out=flat(kab), in0=flat(ka), scalar=-1.0, in1=flat(be),
                                                 op0=ALU.mult, op1=ALU.mult))
                    gmb = gm[:].unsqueeze(2).broadcast_to([P, NC * H, C])
                    own(dve.tensor_tensor(rows(kcb), rows(kab), gmb, ALU.mult))
                    own(dve.tensor_tensor(wq[:, :, :, 1, :].rearrange("p c h i -> p (c h) i"), rows(qa), gmb,
                                          ALU.mult))
                    dve.tensor_tensor(rows(kd), rows(kb), rows(ea)[:, :, 7:8].broadcast_to([P, NC * H, C]),
                                      ALU.mult).then_inc(q["kqv_ready"], 1)
                    dve.wait_ge(q["m_mm"], g + 1)
                    dve.sem_inc(q["dve_turn"], 1)
                    for t, n, mask in ((mt, Q, s.rows_first), (mm, K, s.rows_last), (bt, DRV, s.rows_to)):
                        own(dve.copy_predicated(t[:], mask.bitcast(U32).unsqueeze(1).broadcast_to([P, NC, 64]),
                                                bank_ci(n)))
                    dve.tensor_tensor(imt[:], mt[:], s.ident64.unsqueeze(1).broadcast_to([P, NC, 64]), ALU.add)\
                       .then_inc(q["m_ready"], 1)
                    dve.wait_ge(q["m4_mm"], g + 1)
                    dve.wait_ge(q["m_ready"], g + 1)
                    dve.tensor_tensor(p1[:], bank_ci(DRV), imt[:], ALU.add).then_inc(q["p1_ready"], 1)
                    dve.wait_ge(q["tt_mm"], g + 1)
                    dve.wait_ge(q["p1_ready"], g + 1)
                    dve.tensor_tensor(tt[:], bank_ci(Q), p1[:], ALU.add).then_inc(q["tt_ready"], 1)
                    dve.wait_ge(q["wq_ready"], g + 1)
                    for n in range(NC):
                        xq = ps[:, 3 * (n % 2), 0:2 * 64].rearrange("p (h k i) -> p h k i", h=H, k=2)
                        dve.wait_ge(q["xq_mm"], g * NC + n + 1)
                        dve.tensor_tensor(ut[:].rearrange("p (h i) -> p h i", h=H), xq[:, :, 0, :],
                                          u0[:, n, :].rearrange("p (h i) -> p h i", h=H), ALU.add)\
                           .then_inc(q["ut_ready"], 1)
                        own(dve.tensor_tensor(sd[:], S[:], p8[:, n, :].unsqueeze(2).broadcast_to([P, H, DK]),
                                              ALU.mult))
                        dve.wait_ge(q["ur_mm"], g * NC + n + 1)
                        dve.tensor_tensor(ux[:], ps[:, K, 0:64].unsqueeze(1).broadcast_to([P, H, DK]),
                                          s.head_mask.unsqueeze(2).broadcast_to([P, H, DK]), ALU.mult)\
                           .then_inc(q["ux_ready"], 1)
                        dve.wait_ge(q["ds_mm"], g * NC + n + 1)
                        dve.tensor_tensor(S[:].rearrange("p h v -> p (h v)"), sd[:].rearrange("p h v -> p (h v)"),
                                          bank(V), ALU.add).then_inc(q["s_ready"], 1)
                        dve.wait_ge(q["s_ready"], g * NC + n + 2)
                    dve.wait_ge(q["orms"], g + 1)
                    own(dve.tensor_tensor(flat(t1), ot[:].rearrange("p c i -> p (c i)"), rn[:, 0, :], ALU.mult))
                    dve.tensor_tensor(t1[:], t1[:], per_head(norm_w), ALU.mult).then_inc(q["y_ready"], 1)
                    dve.wait_ge(q["wo_mm"], g + 1)

def gate_and_ff(nc, s):
    a, T, NB, BL, ps, mod = s.a, s.T, s.NB, s.BL, s.ps, s.mod
    R = a["L0_attn_Wu1"].shape[1]
    FF = a["L0_attn_Wff1"].shape[1]
    FK = FF // P
    NU = 2 * NB
    with ExitStack() as c:
        w1 = sbuf(nc, c, "gf_values", [P, 2, T])
        w2 = sbuf(nc, c, "gf_factors", [P, 2, T])
        wu1 = sbuf(nc, c, "gf_wu1", [P, R])
        wu2 = sbuf(nc, c, "gf_wu2", [R, P])
        vecs = sbuf(nc, c, "gf_vectors", [P, 3])
        wff = sbuf(nc, c, "gf_wff13", [P, 2, FF])
        wff2 = sbuf(nc, c, "gf_wff2", [P, FK, P])
        act1 = sbuf(nc, c, "gf_act", [P, FK, BL])
        up = sbuf(nc, c, "gf_up", [P, FK, BL])
        q = signals(nc, c, "gf", "w_in mm pre sig u_ready y_ready squares rms z_ready ff_mm ff_pre ff_sig ff_ready "
                                 "ff_out x_ready sums centered squares2 rstd dve act")
        banks = halves(s)
        blk = lambda t, b: t[:, b, :].rearrange("p (n l) -> p n l", l=BL)
        f_a = ps[:, 0:FK, 0:BL]
        f_b = ps[:, FK:2 * FK, 0:BL]
        assert FK == 4
        with nc.Block() as block:
            @block.sync
            def _(sp):
                for dst, src in ((wu1[:], a["L0_attn_Wu1"]), (wu2[:], a["L0_attn_Wu2"]),
                                 (vecs[0:R, 0:1], a["L0_attn_bu1"].unsqueeze(1)),
                                 (vecs[:, 1:2], a["L0_attn_bu2"].unsqueeze(1)),
                                 (vecs[:, 2:3], a["L0_attn_ff_norm_w"].unsqueeze(1)),
                                 (wff[:, 0, :], a["L0_attn_Wff1"]), (wff[:, 1, :], a["L0_attn_Wff3"]),
                                 (wff2[:], a["L0_attn_Wff2"].rearrange("(k p) n -> p k n", p=P))):
                    sp.dma_start(dst, src).then_inc(q["w_in"], 16)

            @block.tensor
            def _(pe):
                def over(b, lhs, src, rows=P):
                    for n in range(NB):
                        ins = pe.matmul(ps[0:rows, 4 * b + n, 0:BL], lhs, src[0:lhs.shape[0], b, BL * n:BL * n + BL],
                                        start=True, stop=True)
                    return ins

                pe.wait_ge(q["w_in"], 8 * 16)
                for b in range(2):
                    over(b, wu1[:], s.h, R).then_inc(q["mm"], 1)
                for b in range(2):
                    pe.wait_ge(q["u_ready"], b + 1)
                    over(b, wu2[:], w1).then_inc(q["mm"], 1)
                for b in range(2):
                    pe.wait_ge(q["squares"], b + 1)
                    over(b, s.ones[:], w2).then_inc(q["mm"], 1)
                for u in range(NU):
                    b, n = divmod(u, NB)
                    pe.wait_ge(q["z_ready"], b + 1)
                    pe.wait_ge(q["z_ready"], 2)
                    if u:
                        pe.wait_ge(q["ff_out"], u)
                    for m in range(2):
                        for k in range(FK):
                            ins = pe.matmul(ps[:, FK * m + k, 0:BL], wff[:, m, P * k:P * k + P],
                                            w2[:, b, BL * n:BL * n + BL], start=True, stop=True)
                    ins.then_inc(q["ff_mm"], 1)
                    pe.wait_ge(q["ff_ready"], u + 1)
                    for k in range(FK):
                        ins = pe.matmul(ps[:, 0, 0:BL], wff2[:, k, :], up[:, k, :], start=(k == 0),
                                        stop=(k == FK - 1))
                    ins.then_inc(q["ff_mm"], 1)
                for b in range(2):
                    pe.wait_ge(q["x_ready"], 2)
                    over(b, s.ones[:], s.x).then_inc(q["sums"], 1)
                for b in range(2):
                    pe.wait_ge(q["squares2"], b + 1)
                    over(b, s.ones[:], w2).then_inc(q["sums"], 1)

            @block.scalar
            def _(act):
                own = Link(act, q["act"])

                def sigmoid(t):
                    own(act.activation(t, t, ACT.Exp, scale=-1.0))
                    own(act.activation(t, t, ACT.Ln, bias=1.0))
                    return act.activation(t, t, ACT.Exp, scale=-1.0)

                for b in range(2):
                    act.wait_ge(q["pre"], b + 1)
                    sigmoid(w2[0:R, b, :]).then_inc(q["sig"], 1)
                for b in range(2):
                    act.wait_ge(q["pre"], b + 3)
                    sigmoid(w2[:, b, :]).then_inc(q["sig"], 1)
                for b in range(2):
                    act.wait_ge(q["y_ready"], b + 1)
                    act.activation(w2[:, b, :], w1[:, b, :], ACT.Square).then_inc(q["squares"], 1)
                for b in range(2):
                    act.wait_ge(q["mm"], b + 5)
                    own(act.activation(blk(w2, b), banks[b], ACT.Ln, scale=1.0 / D, bias=1e-6))
                    act.activation(w2[:, b, :], w2[:, b, :], ACT.Exp, scale=-0.5).then_inc(q["rms"], 1)
                for u in range(NU):
                    act.wait_ge(q["ff_pre"], u + 1)
                    sigmoid(act1[:]).then_inc(q["ff_sig"], 1)
                for b in range(2):
                    act.wait_ge(q["centered"], b + 1)
                    act.activation(w2[:, b, :], w1[:, b, :], ACT.Square).then_inc(q["squares2"], 1)
                for b in range(2):
                    act.wait_ge(q["sums"], b + 3)
                    own(act.activation(blk(w2, b), banks[b], ACT.Ln, scale=1.0 / D, bias=1e-5))
                    act.activation(w2[:, b, :], w2[:, b, :], ACT.Exp, scale=-0.5).then_inc(q["rstd"], 1)

            @block.vector
            def _(dve):
                own = Link(dve, q["dve"])
                dve.wait_ge(q["w_in"], 8 * 16)
                for b in range(2):
                    dve.wait_ge(q["mm"], b + 1)
                    own(dve.tensor_scalar(blk(w1, b)[0:R], banks[b][0:R], vecs[0:R, 0:1], None, ALU.add))
                    dve.tensor_scalar(w2[0:R, b, :], w1[0:R, b, :], SIG_MIN, None, ALU.max).then_inc(q["pre"], 1)
                for b in range(2):
                    dve.wait_ge(q["sig"], b + 1)
                    dve.tensor_tensor(w1[0:R, b, :], w1[0:R, b, :], w2[0:R, b, :], ALU.mult).then_inc(q["u_ready"], 1)
                for b in range(2):
                    dve.wait_ge(q["mm"], b + 3)
                    dve.tensor_scalar(blk(w2, b), banks[b], vecs[:, 1:2], SIG_MIN, ALU.add, ALU.max)\
                       .then_inc(q["pre"], 1)
                for b in range(2):
                    dve.wait_ge(q["sig"], b + 3)
                    own(dve.tensor_tensor(w1[:, b, :], s.y[:, b, :], w2[:, b, :], ALU.mult))
                    dve.tensor_tensor(w1[:, b, :], w1[:, b, :], s.h[:, b, :], ALU.add).then_inc(q["y_ready"], 1)
                for b in range(2):
                    dve.wait_ge(q["rms"], b + 1)
                    dve.wait_ge(q["y_ready"], b + 1)
                    dve.scalar_tensor_tensor(out=w2[:, b, :], in0=w1[:, b, :], scalar=vecs[:, 2:3],
                                             in1=w2[:, b, :], op0=ALU.mult, op1=ALU.mult).then_inc(q["z_ready"], 1)
                for u in range(NU):
                    b, n = divmod(u, NB)
                    dve.wait_ge(q["ff_mm"], 2 * u + 1)
                    dve.tensor_scalar(act1[:], f_a, SIG_MIN, None, ALU.max).then_inc(q["ff_pre"], 1)
                    own(dve.tensor_copy(up[:], f_b))
                    own(dve.tensor_tensor(up[:], up[:], f_a, ALU.mult))
                    dve.wait_ge(q["ff_sig"], u + 1)
                    dve.tensor_tensor(up[:], up[:], act1[:], ALU.mult).then_inc(q["ff_ready"], 1)
                    dve.wait_ge(q["ff_mm"], 2 * u + 2)
                    dve.tensor_tensor(w1[:, b, BL * n:BL * n + BL], w1[:, b, BL * n:BL * n + BL],
                                      ps[:, 0, 0:BL], ALU.add).then_inc(q["ff_out"], 1)
                dve.wait_ge(q["ff_out"], NU)
                for b in range(2):
                    dve.scalar_tensor_tensor(out=s.x[:, b, :], in0=w1[:, b, :], scalar=mod[:, GATE_A, b:b + 1],
                                             in1=s.x[:, b, :], op0=ALU.mult, op1=ALU.add).then_inc(q["x_ready"], 1)
                dve.wait_ge(q["x_ready"], 2)
                for b in range(2):
                    dve.wait_ge(q["sums"], b + 1)
                    dve.scalar_tensor_tensor(out=blk(w1, b), in0=banks[b], scalar=-1.0 / D, in1=blk(s.x, b),
                                             op0=ALU.mult, op1=ALU.add).then_inc(q["centered"], 1)
                for b in range(2):
                    dve.wait_ge(q["rstd"], b + 1)
                    dve.wait_ge(q["centered"], b + 1)
                    own(dve.tensor_tensor(w1[:, b, :], w1[:, b, :], w2[:, b, :], ALU.mult))
                    own(dve.tensor_scalar(s.xa[:, XPAD + T * b:XPAD + T * b + T], w1[:, b, :],
                                          mod[:, SC_B, b:b + 1], mod[:, SH_B, b:b + 1], ALU.mult, ALU.add))
                own(dve.memset(s.xa[:, 0:XPAD], 0.0))



def windowed_layers(nc, s, out):
    a, T, NB, BL, ps, mod, xa = s.a, s.T, s.NB, s.BL, s.ps, s.mod, s.xa
    DEPTH = a["wqkv"].shape[0]
    INNER = HEADS * DH
    FI = a["w1"].shape[2] // 2
    NT = 2 * T // TILE
    NU = 2 * NB
    CH = [min(P, FI - P * k) for k in range((FI + P - 1) // P)]
    NCH = len(CH)
    NS = NCH * NU
    assert NCH == 3
    with ExitStack() as c:
        def sb(name, shape):
            return sbuf(nc, c, name, shape)

        xb = sb("xb", [P, XPAD + 2 * T])
        fs = sb("ff_values", [P, 2, T])
        fq = sb("ff_factors", [P, 2, T])
        tabs = sb("rotary_tables", [P, NT, 4 * DH])
        masks = sb("masks", [P, NT, 2 * WIN])
        cols = sb("tile_columns", [P, NT + 1])
        wqkv = sb("wqkv", [P, 3 * INNER])
        wo = sb("wo_pairs", [P, PAIRS, D])
        scales = sb("qk_scales", [P, 4 * DH])
        w1 = sb("w1", [P, 2 * FI])
        w2 = sb("w2", [P, NCH, D])
        vecs = sb("layer_vectors", [P, 9])
        xs = sb("xs", [P, HALO + TILE])
        xr = sb("xr", [P, 2, TILE])
        tab = sb("tab", [P, 4 * DH])
        mask = sb("mask", [P, 2 * WIN])
        sq = fs[:].rearrange("p b t -> p (b t)")[:, 0:2 * INNER] if T >= INNER else sb("sq", [P, 2 * INNER])[:]
        rn = sb("rn", [P, 2 * HEADS])
        qr = sb("qr", [P, INNER])
        kr = sb("kr", [P, INNER])
        t2 = sb("t2", [P, INNER])
        qt = sb("qt", [P, PAIRS, TILE])
        kt = sb("kt", [P, PAIRS, HALO + TILE])
        vs = sb("vs", [P, 4, PAIRS * DH])
        s1 = sb("s1", [P, 2, PAIRS, 2 * WIN])
        mx = sb("mx", [P, 2, PAIRS])
        pr = sb("pr", [P, PAIRS, 2, 2 * WIN])
        rs = sb("rs", [P, 2 * PAIRS])
        pt = sb("pt", [P, PAIRS, TILE])
        ot = sb("ot", [P, PAIRS, TILE])
        gel = sb("gel", [P, 3, BL])
        hid = sb("hid", [P, 3, BL])
        q = signals(nc, c, "wl", "tabs_in attn_w_in ff_w_in cleared xs tab mask sim qk pt_mm o_mm v_mm q_t k_t wo_mm exp "
                                 "squares rnorm pt_in o_in v_in qk_in smax p_ready ssq rotq rotk xb_ready "
                                 "fs_ready ln_sums centered squares2 rstd xn_ready w1_mm gelu hid_ready w2_mm "
                                 "xa_ready pe_turn pool_turn dve act pool last out_done")
        blk = lambda t, b: t[:, b, :].rearrange("p (n l) -> p n l", l=BL)
        banks = halves(s)
        two = lambda n: ps[:, n:n + 2, :]
        Q0, K0, S0, O0 = 0, 2, 4, 6
        heads = lambda t: t.rearrange("p (h d) -> p h d", d=DH)

        def tiles(eng, base, body):
            body(None, base, -1)
            with eng.Fori(0, NT - 1) as t:
                body(base + t, base + t + 1, t)
            body(base + (NT - 1), None, NT - 1)

        with nc.Block() as block:
            @block.sync
            def _(sp):
                sp.dma_start(tabs[:], s.const["tabs"]).then_inc(q["tabs_in"], 16)
                sp.dma_start(masks[:], s.const["masks"]).then_inc(q["tabs_in"], 16)
                sp.dma_start(cols[:], s.const["cols"]).then_inc(q["tabs_in"], 16)
                with sp.Fori(0, DEPTH) as l:
                    sp.wait_ge(q["wo_mm"], l * NT)
                    sp.wait_ge(q["tab"], l * NT)
                    row = lambda t: a[t][bass.ds(l, 1)]
                    sp.dma_start(wqkv[:], row("wqkv").rearrange("a p n -> (a p) n")).then_inc(q["attn_w_in"], 16)
                    sp.dma_start(wo[:], row("wo").rearrange("a (m r) n -> (a r) m n", r=P))\
                      .then_inc(q["attn_w_in"], 16)
                    sp.dma_start(scales[:], row("scales").broadcast_to([P, 4 * DH])).then_inc(q["attn_w_in"], 16)
                    sp.wait_ge(q["xa_ready"], l * NU)
                    sp.dma_start(w1[:], row("w1").rearrange("a p n -> (a p) n")).then_inc(q["ff_w_in"], 16)
                    sp.dma_start(w2[:], row("w2").rearrange("a (k p) n -> (a p) k n", p=P)).then_inc(q["ff_w_in"], 16)
                    sp.dma_start(vecs[:], row("vecs").rearrange("a p n -> (a p) n")).then_inc(q["ff_w_in"], 16)
                sp.wait_ge(q["last"], 2)
                for b in range(2):
                    sp.dma_start(out[:, b, :], fs[:, b, :]).then_inc(q["out_done"], 16)
                sp.wait_ge(q["out_done"], 32)

            @block.gpsimd
            def _(pool):
                own = Link(pool, q["pool"])

                def hold():
                    pool.sem_inc(q["pool_turn"], 1)

                pool.wait_ge(q["tabs_in"], 48)
                with pool.Fori(0, DEPTH) as l:
                    pool.wait_ge(q["attn_w_in"], (l + 1) * 48)
                    pool.wait_ge(q["xa_ready"], l * NU)
                    hold()

                    def body(cb, ca, t):
                        own.restart()
                        if cb is not None:
                            pool.wait_ge(q["smax"], 2 * cb)
                            hold()
                            pool.tensor_copy(mask[:].unsqueeze(1), masks[:, bass.ds(t, 1), :]).then_inc(q["mask"], 1)
                        if ca is not None:
                            pool.wait_ge(q["v_mm"], 2 * ca)
                            hold()
                            own(pool.tensor_copy(xs[0:64, :], xa[0:64, bass.ds((t + 1) * TILE + 1, HALO + TILE)]))
                            own(pool.tensor_copy(xs[64:128, :], xa[64:128, bass.ds((t + 1) * TILE, HALO + TILE)]))
                            own(pool.tensor_tensor(xs[64:128, HALO:HALO + 1], xs[64:128, HALO:HALO + 1],
                                                   cols[64:128, bass.ds(t + 1, 1)], ALU.mult))
                            own(pool.tensor_copy(xr[:, 0, 0:64], xs[:, 96:160]))
                            own(pool.tensor_copy(xr[:, 0, 64:128], xs[:, 32:96]))
                            own(pool.tensor_copy(xr[:, 1, 0:64], xs[:, 64:128]))
                            pool.tensor_copy(xr[:, 1, 64:128], xs[:, 0:64]).then_inc(q["xs"], 1)
                            pool.wait_ge(q["rotk"], ca)
                            pool.tensor_tensor(tab[:].unsqueeze(1), tabs[:, bass.ds(t + 1, 1), :],
                                               scales[:].unsqueeze(1), ALU.mult).then_inc(q["tab"], 1)

                    tiles(pool, l * NT, body)
                    own.restart()
                    pool.wait_ge(q["xb_ready"], (l + 1) * NT)
                    pool.wait_ge(q["xs"], (l + 1) * NT)
                    hold()
                    for b in range(2):
                        x0 = XPAD + T * b
                        own(pool.tensor_copy(fs[0:64, b, :], xb[0:64, x0:x0 + T]))
                        own(pool.memset(fs[64:128, b, 0:1], 0.0))
                        pool.tensor_copy(fs[64:128, b, 1:T], xb[64:128, x0:x0 + T - 1]).then_inc(q["fs_ready"], 1)

            @block.tensor
            def _(pe):
                def hold():
                    pe.sem_inc(q["pe_turn"], 1)

                def scores(cb):
                    pe.wait_ge(q["qk_in"], 2 * cb + 2)
                    hold()
                    for f in range(2):
                        for m in range(PAIRS):
                            for w in range(TILE // WIN):
                                e = (f + w // 2) % 2
                                ins = pe.matmul(ps[WIN * w:WIN * w + WIN, S0 + f, 64 * m:64 * m + 64],
                                                qt[64 * e:64 * e + 64, m, WIN * w:WIN * w + WIN],
                                                kt[64 * e:64 * e + 64, m, WIN * w:WIN * w + 2 * WIN],
                                                start=True, stop=True)
                        ins.then_inc(q["sim"], 1)

                def project_qk(ca):
                    pe.wait_ge(q["xs"], ca + 1)
                    for m in range(4):
                        ins = pe.matmul(ps[:, Q0 + m, :], xs[:, HALO:HALO + TILE], wqkv[:, 512 * m:512 * m + 512],
                                        start=True, stop=True)
                        if m % 2:
                            ins.then_inc(q["qk"], 1)

                def transpose_probs(cb):
                    pe.wait_ge(q["p_ready"], cb + 1)
                    for m in range(PAIRS):
                        ins = pe.transpose(ps[:, S0 + m // 4, TILE * (m % 4):TILE * (m % 4) + TILE],
                                           pr[:, m, :, :].rearrange("p f j -> p (f j)"), s.ident)
                    ins.then_inc(q["pt_mm"], 1)

                def weigh_values(cb):
                    pe.wait_ge(q["pt_in"], cb + 1)
                    hold()
                    for m in range(PAIRS):
                        for w in range(TILE // WIN):
                            for e in range(2):
                                f = (e + w // 2) % 2
                                v = 2 * (1 - w % 2) + e
                                o = 64 * m + WIN * (w % 2)
                                ins = pe.matmul(ps[64 * e:64 * e + 64, O0 + w // 2, o:o + WIN],
                                                vs[64 * f:64 * f + 64, v, DH * m:DH * m + DH],
                                                pt[64 * f:64 * f + 64, m, WIN * w:WIN * w + WIN],
                                                start=True, stop=True)
                    ins.then_inc(q["o_mm"], 1)

                def project_v(ca):
                    wv = wqkv[:, 2 * INNER:3 * INNER].rearrange("p (m e d) -> p e m d", e=2, d=DH)
                    for r, (even, odd) in enumerate(((xs[:, HALO:HALO + TILE], xr[:, 0, :]),
                                                     (xs[:, 0:TILE], xr[:, 1, :]))):
                        if r:
                            pe.wait_ge(q["v_in"], 2 * ca + 1)
                        for e, x in enumerate((even, odd)):
                            ins = pe.matmul(ps[:, S0 + e, :].rearrange("p (m d) -> p m d", d=DH), x, wv[:, e],
                                            start=True, stop=True)
                        ins.then_inc(q["v_mm"], 1)

                def transpose_qk(ca):
                    for src, bank0, ready, done in ((qr, S0, q["rotq"], q["q_t"]), (kr, O0, q["rotk"], q["k_t"])):
                        pe.wait_ge(ready, ca + 1)
                        if src is qr:
                            pe.wait_ge(q["v_in"], 2 * ca + 2)
                        for m in range(PAIRS):
                            ins = pe.transpose(ps[:, bank0 + m // 4, TILE * (m % 4):TILE * (m % 4) + TILE],
                                               src[:, P * m:P * m + P], s.ident)
                        ins.then_inc(done, 1)

                def body(cb, ca, t):
                    if cb is not None:
                        scores(cb)
                    if ca is not None:
                        pe.wait_ge(q["xb_ready"], ca if cb is None else cb)
                        project_qk(ca)
                    if cb is not None:
                        transpose_probs(cb)
                        weigh_values(cb)
                    if ca is not None:
                        project_v(ca)
                    if cb is not None:
                        pe.wait_ge(q["o_in"], cb + 1)
                    if ca is not None:
                        transpose_qk(ca)
                    if cb is not None:
                        for m in range(PAIRS):
                            ins = pe.matmul(ps[:, Q0, 0:TILE], wo[:, m, :], ot[:, m, :], start=(m == 0),
                                            stop=(m == PAIRS - 1))
                        ins.then_inc(q["wo_mm"], 1)

                pe.wait_ge(q["cleared"], 1)
                with pe.Fori(0, DEPTH) as l:
                    pe.wait_ge(q["attn_w_in"], (l + 1) * 48)
                    tiles(pe, l * NT, body)
                    pe.wait_ge(q["xb_ready"], (l + 1) * NT)
                    for n, (ready, src) in enumerate(((q["fs_ready"], fs), (q["squares2"], fq))):
                        for b in range(2):
                            pe.wait_ge(ready, 2 * l + b + 1)
                            for k in range(NB):
                                ins = pe.matmul(ps[:, 4 * b + k, 0:BL], s.ones[:], src[:, b, BL * k:BL * k + BL],
                                                start=True, stop=True)
                            ins.then_inc(q["ln_sums"], 1)
                    pe.wait_ge(q["ff_w_in"], (l + 1) * 48)
                    pe.wait_ge(q["xn_ready"], 2 * l + 2)
                    for k in range(NS + 2):
                        if k < NS:
                            (u, j), m = divmod(k, NCH), CH[k % NCH]
                            b, n = divmod(u, NB)
                            if k >= 3:
                                pe.wait_ge(q["hid_ready"], l * NS + k - 2)
                            for g in range(2):
                                ins = pe.matmul(ps[0:m, 2 * (k % 3) + g, 0:BL], w1[:, FI * g + P * j:FI * g + P * j + m],
                                                fs[:, b, BL * n:BL * n + BL], start=True, stop=True)
                            ins.then_inc(q["w1_mm"], 1)
                        if k >= 2:
                            r = k - 2
                            (u, j), m = divmod(r, NCH), CH[r % NCH]
                            if j == 0 and u >= 2:
                                pe.wait_ge(q["xa_ready"], l * NU + u - 1)
                            pe.wait_ge(q["hid_ready"], l * NS + r + 1)
                            pe.matmul(ps[:, 6 + u % 2, 0:BL], w2[0:m, j, :], hid[0:m, r % 3, :], start=(j == 0),
                                      stop=(j == NCH - 1)).then_inc(q["w2_mm"], 1)

            @block.scalar
            def _(act):
                own = Link(act, q["act"])

                def body(cb, ca, t):
                    own.restart()
                    if cb is not None:
                        act.wait_ge(q["pt_mm"], cb)
                        for f in range(2):
                            act.wait_ge(q["smax"], 2 * cb + f + 1)
                            act.activation(pr[:, :, f, :], s1[:, f, :, :], ACT.Exp, scale=DH ** 0.5)\
                               .then_inc(q["exp"], 1)
                    if ca is not None:
                        act.wait_ge(q["ssq"], ca)
                        for n in range(2):
                            act.wait_ge(q["qk"], 2 * ca + n + 1)
                            act.activation(sq[:, INNER * n:INNER * n + INNER],
                                           two(Q0 + 2 * n).rearrange("p a n -> p (a n)"), ACT.Square)\
                               .then_inc(q["squares"], 1)
                        act.wait_ge(q["ssq"], ca + 1)
                        own(act.activation(rn[:], rn[:], ACT.Ln, scale=2.0 ** 20))
                        own(act.activation(rn[:], rn[:], ACT.Exp, scale=-0.5))
                        act.activation(rn[:], rn[:], ACT.Copy, scale=2.0 ** 10).then_inc(q["rnorm"], 1)
                    if cb is not None:
                        act.wait_ge(q["pt_mm"], cb + 1)
                        act.activation(pt[:].rearrange("p (a m) t -> p a (m t)", a=2), two(S0), ACT.Copy)\
                           .then_inc(q["pt_in"], 1)
                        act.wait_ge(q["o_mm"], cb + 1)
                        for w in range(2):
                            ins = act.activation(ot[:, :, 64 * w:64 * w + 64],
                                                 ps[:, O0 + w, :].rearrange("p (m t) -> p m t", t=64), ACT.Copy)
                            if w == 0:
                                own(ins)
                        ins.then_inc(q["o_in"], 1)
                    if ca is not None:
                        for r in range(2):
                            act.wait_ge(q["v_mm"], 2 * ca + r + 1)
                            act.activation(vs[:, 2 * r:2 * r + 2, :], two(S0), ACT.Copy).then_inc(q["v_in"], 1)
                        act.wait_ge(q["q_t"], ca + 1)
                        act.activation(qt[:].rearrange("p (a m) t -> p a (m t)", a=2), two(S0), ACT.Copy)\
                           .then_inc(q["qk_in"], 1)
                        own(act.activation(kt[:, :, 0:HALO], kt[:, :, TILE:TILE + HALO], ACT.Copy,
                                           scale=cols[:, NT:NT + 1]))
                        act.wait_ge(q["k_t"], ca + 1)
                        for k in range(2):
                            ins = act.activation(kt[:, 4 * k:4 * k + 4, HALO:HALO + TILE],
                                                 ps[:, O0 + k, :].rearrange("p (m t) -> p m t", t=TILE), ACT.Copy)
                            if k == 0:
                                own(ins)
                        ins.then_inc(q["qk_in"], 1)
                        act.wait_ge(q["qk_in"], 2 * ca + 2)

                act.wait_ge(q["cleared"], 1)
                act.wait_ge(q["tabs_in"], 48)
                with act.Fori(0, DEPTH) as l:
                    act.preload_act_table_set(LN_EXP)
                    tiles(act, l * NT, body)
                    own.restart()
                    for b in range(2):
                        act.wait_ge(q["centered"], 2 * l + b + 1)
                        act.activation(fq[:, b, :], fs[:, b, :], ACT.Square).then_inc(q["squares2"], 1)
                    for b in range(2):
                        act.wait_ge(q["ln_sums"], 4 * l + b + 3)
                        own(act.activation(blk(fq, b), banks[b], ACT.Ln, scale=1.0 / D, bias=1e-5))
                        act.activation(fq[:, b, :], fq[:, b, :], ACT.Exp, scale=-0.5).then_inc(q["rstd"], 1)
                    act.wait_ge(q["ff_w_in"], (l + 1) * 48)
                    for k in range(NS):
                        j, m = k % NCH, CH[k % NCH]
                        act.wait_ge(q["w1_mm"], l * NS + k + 1)
                        act.activation(gel[0:m, k % 3, :], ps[0:m, 2 * (k % 3) + 1, 0:BL], ACT.Gelu,
                                       bias=vecs[0:m, 6 + j:7 + j]).then_inc(q["gelu"], 1)

            @block.vector
            def _(dve):
                own = Link(dve, q["dve"])

                def rotate(src0, dst, used, table, norm, ready, ca):
                    src = heads(two(src0).rearrange("p a n -> p (a n)"))
                    tb = lambda lo, n: tab[:, table + lo:table + lo + n].unsqueeze(1).broadcast_to([P, HEADS, n])
                    own(dve.tensor_tensor(heads(dst[:]), src, tb(0, DH), ALU.mult))
                    t2h = heads(t2[:])
                    own(dve.tensor_tensor(t2h[:, :, 0:32], src[:, :, 32:64], tb(DH, 32), ALU.mult))
                    own(dve.tensor_tensor(t2h[:, :, 32:64], src[:, :, 0:32], tb(DH + 32, 32), ALU.mult))
                    own(dve.tensor_tensor(dst[:], dst[:], t2[:], ALU.add))
                    dve.tensor_tensor(heads(dst[:]), heads(dst[:]),
                                      rn[:, norm:norm + HEADS].unsqueeze(2).broadcast_to([P, HEADS, DH]), ALU.mult)\
                       .then_inc(ready, 1)

                def body(cb, ca, t):
                    own.restart()
                    if cb is not None:
                        dve.wait_ge(q["mask"], cb + 1)
                        for f in range(2):
                            dve.wait_ge(q["sim"], 2 * cb + f + 1)
                            sim = ps[:, S0 + f, :].rearrange("p (m j) -> p m j", j=64)
                            own(dve.tensor_tensor(s1[:, f], sim, mask[:].unsqueeze(1).broadcast_to([P, PAIRS, 64]),
                                                  ALU.add))
                            own(dve.tensor_reduce(mx[:, f, :], s1[:, f], AX_X, ALU.max))
                            dve.tensor_tensor(s1[:, f], s1[:, f],
                                              mx[:, f, :].unsqueeze(2).broadcast_to([P, PAIRS, 64]), ALU.subtract)\
                               .then_inc(q["smax"], 1)
                    if ca is not None:
                        dve.wait_ge(q["squares"], 2 * ca + 2)
                        dve.wait_ge(q["rotk"], ca)
                        own(dve.tensor_reduce(rn[:], heads(sq), AX_X, ALU.add))
                        dve.tensor_scalar(rn[:], rn[:], 1e-24, None, ALU.max).then_inc(q["ssq"], 1)
                    if cb is not None:
                        dve.wait_ge(q["exp"], 2 * cb + 2)
                        prh = pr[:].rearrange("p m f j -> p (m f) j")
                        own(dve.tensor_reduce(rs[:], prh, AX_X, ALU.add))
                        own(dve.reciprocal(rs[:], rs[:]))
                        dve.tensor_tensor(prh, prh, rs[:].unsqueeze(2).broadcast_to([P, 2 * PAIRS, 64]), ALU.mult)\
                           .then_inc(q["p_ready"], 1)
                    if ca is not None:
                        dve.wait_ge(q["rnorm"], ca + 1)
                        dve.wait_ge(q["tab"], ca + 1)
                        dve.wait_ge(q["k_t"], ca)
                        rotate(Q0, qr, q["q_t"], 0, 0, q["rotq"], ca)
                        dve.wait_ge(q["rotq"], ca + 1)
                        rotate(K0, kr, q["k_t"], 2 * DH, HEADS, q["rotk"], ca)
                    if cb is not None:
                        x0 = t * TILE + XPAD
                        dve.wait_ge(q["wo_mm"], cb + 1)
                        dve.tensor_tensor(xb[:, bass.ds(x0, TILE)], xa[:, bass.ds(x0, TILE)], ps[:, Q0, 0:TILE],
                                          ALU.add).then_inc(q["xb_ready"], 1)

                own(dve.memset(xb[:, 0:XPAD], 0.0))
                dve.memset(kt[:], 0.0).then_inc(q["cleared"], 1)
                with dve.Fori(0, DEPTH) as l:
                    tiles(dve, l * NT, body)
                    own.restart()
                    dve.wait_ge(q["ff_w_in"], (l + 1) * 48)
                    for b in range(2):
                        dve.wait_ge(q["ln_sums"], 4 * l + b + 1)
                        dve.scalar_tensor_tensor(out=blk(fs, b), in0=banks[b], scalar=-1.0 / D, in1=blk(fs, b),
                                                 op0=ALU.mult, op1=ALU.add).then_inc(q["centered"], 1)
                    for b in range(2):
                        dve.wait_ge(q["rstd"], 2 * l + b + 1)
                        own(dve.tensor_tensor(fs[:, b, :], fs[:, b, :], fq[:, b, :], ALU.mult))
                        dve.tensor_scalar(fs[:, b, :], fs[:, b, :], vecs[:, 0:1], vecs[:, 1:2], ALU.mult, ALU.add)\
                           .then_inc(q["xn_ready"], 1)
                    for k in range(NS):
                        (u, j), m = divmod(k, NCH), CH[k % NCH]
                        b, n = divmod(u, NB)
                        if k >= 3:
                            dve.wait_ge(q["w2_mm"], l * NS + k - 2)
                        dve.wait_ge(q["gelu"], l * NS + k + 1)
                        dve.scalar_tensor_tensor(out=hid[0:m, k % 3, :], in0=ps[0:m, 2 * (k % 3), 0:BL],
                                                 scalar=vecs[0:m, 3 + j:4 + j], in1=gel[0:m, k % 3, :],
                                                 op0=ALU.add, op1=ALU.mult).then_inc(q["hid_ready"], 1)
                        if j == NCH - 1:
                            x0 = XPAD + BL * u
                            dve.wait_ge(q["w2_mm"], l * NS + k + 1)
                            dve.scalar_tensor_tensor(out=xa[:, x0:x0 + BL], in0=ps[:, 6 + u % 2, 0:BL],
                                                     scalar=vecs[:, 2:3], in1=xb[:, x0:x0 + BL],
                                                     op0=ALU.add, op1=ALU.add).then_inc(q["xa_ready"], 1)
                    dve.wait_ge(q["xa_ready"], (l + 1) * NU)
                for b in range(2):
                    x0 = XPAD + T * b
                    dve.scalar_tensor_tensor(out=fs[:, b, :], in0=xa[:, x0:x0 + T], scalar=mod[:, GATE_B, b:b + 1],
                                             in1=s.x[:, b, :], op0=ALU.mult, op1=ALU.add).then_inc(q["last"], 1)



INPUTS = """L0_attn_x L0_attn_norm_in_w L0_attn_conv_w L0_attn_conv_b L0_attn_Wq L0_attn_Wk L0_attn_Wv L0_attn_Wo
L0_attn_Wspike L0_attn_Wau L0_attn_bau L0_attn_Wad L0_attn_bad L0_attn_alpha_spike L0_attn_Wbeta L0_attn_bbeta
L0_attn_beta_spike L0_attn_head_norm_w L0_attn_Wu1 L0_attn_bu1 L0_attn_Wu2 L0_attn_bu2 L0_attn_ff_norm_w
L0_attn_Wff1 L0_attn_Wff3 L0_attn_Wff2 L0_c L0_wmod""".split()


TRANSPOSED = {"L0_attn_x": (2, 0, 1), "L0_c": (1, 0), "L0_attn_beta_spike": (0, 2, 1),
              "L0_attn_alpha_spike": (0, 2, 1), "L0_attn_head_norm_w": (1, 0)}


def laid_out(name, x):
    return np.ascontiguousarray(np.transpose(x, TRANSPOSED[name]) if name in TRANSPOSED else x)


def layer_arrays(x):
    def columns(v):
        n = -(-v.shape[1] // P)
        out = np.zeros((v.shape[0], n * P), v.dtype)
        out[:, :v.shape[1]] = v
        return out.reshape(v.shape[0], n, P).transpose(0, 2, 1)

    half, inner = DH // 2, x["L0_ffn_b1"].shape[1] // 2
    w2 = x["L0_ffn_W2"]
    padded = np.zeros((w2.shape[0], -(-inner // P) * P, w2.shape[2]), w2.dtype)
    padded[:, :inner] = w2
    swapped = [np.concatenate([v, v[:, half:], v[:, :half]], axis=1)
               for v in (x["L0_ffn_q_scale"], x["L0_ffn_k_scale"])]
    vecs = [columns(x["L0_ffn_" + n]) for n in ("ln_g", "ln_b", "b2")]
    vecs += [columns(v) for v in (x["L0_ffn_b1"][:, :inner], x["L0_ffn_b1"][:, inner:])]
    return {"wqkv": x["L0_ffn_Wqkv"], "wo": x["L0_ffn_Wo"], "w1": x["L0_ffn_W1"], "w2": padded,
            "scales": np.concatenate(swapped, axis=1), "vecs": np.concatenate(vecs, axis=2)}


def kernel(**inputs):
    import concourse.bacc as bacc
    from concourse.bass_utils import run_bass_kernel_spmd

    nc = bacc.Bacc("TRN2", target_bir_lowering=False, num_devices=1)
    arrays, a, const = {}, {}, {}
    given = {name: laid_out(name, inputs[name]) for name in INPUTS}
    given |= layer_arrays({k: np.asarray(v) for k, v in inputs.items()})
    for name, x in given.items():
        arrays[f"in_{name}"] = x = np.ascontiguousarray(x)
        a[name] = nc.dram_tensor(f"in_{name}", x.shape, mybir.dt.from_np(x.dtype), kind="ExternalInput").ap()
    B, T, _ = inputs["L0_attn_x"].shape
    for name, x in shape_constants(T).items():
        arrays[f"const_{name}"] = x
        const[name] = nc.dram_tensor(f"const_{name}", x.shape, F32, kind="ExternalInput").ap()
    out = nc.dram_tensor("out", (D, B, T), F32, kind="ExternalOutput").ap()
    adaln_block(nc, a, const, out)
    r = run_bass_kernel_spmd(nc, [arrays], core_ids=[0])
    return np.ascontiguousarray(np.transpose(r.results[0]["out"], (1, 2, 0)))
```

```python
from contextlib import ExitStack

import concourse.bass as bass
import numpy as np
from concourse import mybir

F32 = mybir.dt.float32
U32 = mybir.dt.uint32
ALU = mybir.AluOpType
ACT = mybir.ActivationFunctionType
AX_X = mybir.AxisListType.X
LN_EXP = "natural_log_exp_and_others"

P = 128
D = 128
H = 8
DK = 64
C = 8
G = 64
NC = G // C
HEADS = 16
DH = 64
PAIRS = HEADS // 2
WIN = 32
HALO = WIN
XPAD = WIN + 1
TILE = 128
DECAY, THR = 0.9, 0.5
SIG_MIN = -43.0
LOG_DECAY_MAX = 20.7
NEG = -1e30
TINY = 1e-19


def shape_constants(T):
    p = np.arange(P)
    ident = np.eye(P, dtype=np.float32)
    ones_block = (p[:, None] // DK == p[None, :] // DK).astype(np.float32)
    r = p % 64
    col = np.arange(64)
    same = (r[:, None] // C) == (col[None, :] // C)
    rows_first = same & (r[:, None] % C < col[None, :] % C)
    rows_last = same & (r[:, None] % C > col[None, :] % C)
    rows_to = same & (r[:, None] % C <= col[None, :] % C)
    ident64 = (r[:, None] == col[None, :])
    head_of_row = (r[:, None] // C) == np.arange(H)[None, :]
    small = np.concatenate([ident, ones_block, rows_first, rows_last, rows_to, ident64, head_of_row],
                           axis=1).astype(np.float32)
    half = np.arange(0, DH, 2, dtype=np.float32)
    inv_freq = (np.float32(1.0) / np.float32(10000.0) ** (half / np.float32(DH))).astype(np.float32)
    t = np.arange(T, dtype=np.float32)
    freqs = t[:, None] * inv_freq[None, :]
    freqs = np.concatenate([freqs, freqs], -1).astype(np.float32)
    base = (half.astype(np.float64) + 0.4 * DH) / (1.4 * DH)
    base = np.concatenate([base, base])
    power = ((np.arange(T) % TILE) - TILE // 2) / (WIN // 2)
    scale = base[None, :] ** power[:, None]
    sign = np.where(np.arange(DH) < DH // 2, -1.0, 1.0)
    cos, sin = np.cos(freqs), np.sin(freqs)
    tabs = np.stack([cos * scale, sin * scale * sign, cos / scale, sin / scale * sign], axis=1)
    tabs = tabs.reshape(T // TILE, TILE, 4 * DH).transpose(1, 0, 2)
    tabs = np.concatenate([tabs, tabs], axis=1).astype(np.float32)
    i = np.arange(TILE) % WIN
    j = np.arange(WIN)
    m = np.concatenate([np.where(j[None, :] >= i[:, None], 0.0, NEG),
                        np.where(j[None, :] <= i[:, None], 0.0, NEG)], axis=1)
    first = m.copy()
    first[:WIN, :WIN] = NEG
    n = T // TILE
    masks = np.stack([first if k % n == 0 else m for k in range(2 * n)], axis=1).astype(np.float32)
    keep = np.stack([np.full(P, 0.0 if k % n == 0 else 1.0) for k in range(2 * n)], axis=1)
    halo = (base ** (TILE // (WIN // 2)))[p % DH][:, None]
    cols = np.concatenate([keep, halo], axis=1).astype(np.float32)
    return {"small": small, "tabs": np.ascontiguousarray(tabs), "masks": np.ascontiguousarray(masks),
            "cols": np.ascontiguousarray(cols)}


class Shared:
    pass


class Link:

    def __init__(self, eng, sem):
        self.eng, self.sem, self.n = eng, sem, 0

    def __call__(self, ins):
        self.n += 1
        ins.then_inc(self.sem, 1)
        self.eng.wait_ge(self.sem, self.n)

    def restart(self):
        self.eng.sem_clear(self.sem)
        self.n = 0



def sbuf(nc, scope, name, shape, dt=F32):
    return scope.enter_context(nc.sbuf_tensor(name, shape, dt))


def signals(nc, scope, prefix, names):
    return {n: scope.enter_context(nc.semaphore(f"{prefix}_{n}")) for n in names.split()}


def adaln_block(nc, a, const, out):
    T = a["L0_attn_x"].shape[2]
    BL = min(512, T)
    with ExitStack() as top:
        s = Shared()
        s.T, s.BL, s.NB = T, BL, T // BL
        s.a, s.const = a, const
        s.ps = top.enter_context(nc.psum_tensor("ps", [P, 8, 512], F32))
        s.x = sbuf(nc, top, "x_resid", [P, 2, T])
        s.small = sbuf(nc, top, "small_consts", [P, 2 * P + 4 * 64 + H])
        s.ident, s.ones_block = s.small[:, 0:P], s.small[:, P:2 * P]
        s.rows_first, s.rows_last, s.rows_to, s.ident64 = (
            s.small[:, 2 * P + 64 * k:2 * P + 64 * k + 64] for k in range(4))
        s.head_mask = s.small[:, 2 * P + 256:2 * P + 256 + H]
        s.ones = sbuf(nc, top, "ones", [P, P])
        s.mod = sbuf(nc, top, "mod", [P, 6, 2])
        s.xa = sbuf(nc, top, "xa", [P, XPAD + 2 * T])
        modulation(nc, s)
        with ExitStack() as attn:
            s.h = sbuf(nc, attn, "attn_in", [P, 2, T])
            s.y = sbuf(nc, attn, "recurrent_out", [P, 2, T])
            with ExitStack() as conv:
                s.conv = sbuf(nc, conv, "conv_out", [P, 2, T])
                norm_and_conv(nc, s)
                recurrence(nc, s)
            gate_and_ff(nc, s)
        windowed_layers(nc, s, out)


SH_A, SC_A, GATE_A, SH_B, SC_B, GATE_B = range(6)


def modulation(nc, s):
    a, mod = s.a, s.mod
    with ExitStack() as c:
        cT = sbuf(nc, c, "c_t", [P, 2])
        cs = sbuf(nc, c, "c_silu", [P, 2])
        g1 = sbuf(nc, c, "gate_sign", [P, 2])
        g2 = sbuf(nc, c, "gate_size", [P, 2])
        wmod = sbuf(nc, c, "wmod", [P, 6 * P])
        q = signals(nc, c, "mod", "loaded sigmoid silu product dve act")
        with nc.Block() as block:
            @block.sync
            def _(sp):
                sp.dma_start(cT[:], a["L0_c"]).then_inc(q["loaded"], 16)
                sp.dma_start(wmod[:], a["L0_wmod"]).then_inc(q["loaded"], 16)
                sp.dma_start(s.small[:], s.const["small"]).then_inc(q["loaded"], 16)

            @block.scalar
            def _(act):
                act.preload_act_table_set(LN_EXP)
                own = Link(act, q["act"])
                act.wait_ge(q["loaded"], 48)
                own(act.activation(g1[:], cT[:], ACT.Exp, scale=-1.0))
                own(act.activation(g1[:], g1[:], ACT.Ln, bias=1.0))
                act.activation(g1[:], g1[:], ACT.Exp, scale=-1.0).then_inc(q["sigmoid"], 1)

            @block.tensor
            def _(pe):
                pe.wait_ge(q["silu"], 1)
                for k in range(6):
                    ins = pe.matmul(s.ps[:, 0, 2 * k:2 * k + 2], wmod[:, P * k:P * k + P], cs[:],
                                    start=True, stop=True)
                ins.then_inc(q["product"], 1)

            @block.vector
            def _(dve):
                own = Link(dve, q["dve"])
                own(dve.memset(s.ones[:], 1.0))
                dve.wait_ge(q["sigmoid"], 1)
                dve.tensor_tensor(cs[:], cT[:], g1[:], ALU.mult).then_inc(q["silu"], 1)
                dve.wait_ge(q["product"], 1)
                own(dve.tensor_copy(mod[:].rearrange("p k b -> p (k b)"), s.ps[:, 0, 0:12]))
                for k in (SC_A, SC_B):
                    own(dve.tensor_scalar(mod[:, k, :], mod[:, k, :], 1.0, None, ALU.add))
                for k in (GATE_A, GATE_B):
                    own(dve.tensor_scalar(g1[:], mod[:, k, :], 0.0, 2.0, ALU.is_ge, ALU.mult))
                    own(dve.tensor_scalar(g2[:], mod[:, k, :], -1.0, 0.25, ALU.mult, ALU.max))
                    own(dve.tensor_tensor(g2[:], g2[:], mod[:, k, :], ALU.max))
                    own(dve.scalar_tensor_tensor(out=mod[:, k, :], in0=g1[:], scalar=-1.0, in1=g2[:],
                                                 op0=ALU.add, op1=ALU.mult))


def halves(s, bank0=None):
    return [s.ps[:, 4 * b:4 * b + s.NB, 0:s.BL] for b in range(2)]


def norm_and_conv(nc, s):
    a, T, NB, BL, ps, mod = s.a, s.T, s.NB, s.BL, s.ps, s.mod
    with ExitStack() as c:
        w1 = sbuf(nc, c, "nc_values", [P, 2, T])
        w2 = sbuf(nc, c, "nc_factors", [P, 2, T])
        rp = sbuf(nc, c, "nc_rms", [P, 2, T + 3])
        vecs = sbuf(nc, c, "nc_vectors", [P, 6])
        q = signals(nc, c, "nc", "x0_in x1_in vecs_in sums centered squares h squares_h rstd "
                                 "conv sigmoid dve act")
        x_in = [q["x0_in"], q["x1_in"]]
        banks = halves(s)
        blk = lambda t, b: t[:, b, :].rearrange("p (n l) -> p n l", l=BL)
        with nc.Block() as block:
            @block.sync
            def _(sp):
                for b in range(2):
                    sp.dma_start(s.x[:, b, :], a["L0_attn_x"][:, b, :]).then_inc(x_in[b], 16)
                sp.dma_start(vecs[:, 0:1], a["L0_attn_norm_in_w"].unsqueeze(1)).then_inc(q["vecs_in"], 16)
                sp.dma_start(vecs[:, 1:2], a["L0_attn_conv_b"].unsqueeze(1)).then_inc(q["vecs_in"], 16)
                sp.dma_start(vecs[:, 2:6], a["L0_attn_conv_w"].rearrange("c o k -> c (o k)"))\
                  .then_inc(q["vecs_in"], 16)

            @block.tensor
            def _(pe):
                for ready, src in ((None, s.x), (q["squares"], w2), (q["squares_h"], w2)):
                    for b in range(2):
                        pe.wait_ge(ready or x_in[b], b + 1 if ready else 16)
                        for n in range(NB):
                            ins = pe.matmul(ps[:, 4 * b + n, 0:BL], s.ones[:], src[:, b, BL * n:BL * n + BL],
                                            start=True, stop=True)
                        ins.then_inc(q["sums"], 1)

            @block.scalar
            def _(act):
                own = Link(act, q["act"])
                for b in range(2):
                    act.wait_ge(q["centered"], b + 1)
                    act.activation(w2[:, b, :], w1[:, b, :], ACT.Square).then_inc(q["squares"], 1)
                for b in range(2):
                    act.wait_ge(q["sums"], b + 3)
                    own(act.activation(blk(w2, b), banks[b], ACT.Ln, scale=1.0 / D, bias=1e-5))
                    act.activation(w2[:, b, :], w2[:, b, :], ACT.Exp, scale=-0.5).then_inc(q["rstd"], 1)
                for b in range(2):
                    act.wait_ge(q["h"], b + 1)
                    act.activation(w2[:, b, :], s.h[:, b, :], ACT.Square).then_inc(q["squares_h"], 1)
                for b in range(2):
                    act.wait_ge(q["sums"], b + 5)
                    own(act.activation(blk(w2, b), banks[b], ACT.Ln, scale=1.0 / D, bias=1e-6))
                    act.activation(w2[:, b, :], w2[:, b, :], ACT.Exp, scale=-0.5).then_inc(q["rstd"], 1)
                for b in range(2):
                    act.wait_ge(q["conv"], b + 1)
                    own(act.activation(w2[:, b, :], w2[:, b, :], ACT.Exp, scale=-1.0))
                    own(act.activation(w2[:, b, :], w2[:, b, :], ACT.Ln, bias=1.0))
                    act.activation(w2[:, b, :], w2[:, b, :], ACT.Exp, scale=-1.0).then_inc(q["sigmoid"], 1)

            @block.vector
            def _(dve):
                own = Link(dve, q["dve"])
                own(dve.memset(rp[:, :, 0:3], 0.0))
                for b in range(2):
                    dve.wait_ge(q["sums"], b + 1)
                    dve.scalar_tensor_tensor(out=blk(w1, b), in0=banks[b], scalar=-1.0 / D, in1=blk(s.x, b),
                                             op0=ALU.mult, op1=ALU.add).then_inc(q["centered"], 1)
                for b in range(2):
                    dve.wait_ge(q["rstd"], b + 1)
                    dve.wait_ge(q["centered"], b + 1)
                    own(dve.tensor_tensor(w1[:, b, :], w1[:, b, :], w2[:, b, :], ALU.mult))
                    dve.tensor_scalar(s.h[:, b, :], w1[:, b, :], mod[:, SC_A, b:b + 1], mod[:, SH_A, b:b + 1],
                                      ALU.mult, ALU.add).then_inc(q["h"], 1)
                dve.wait_ge(q["vecs_in"], 48)
                for b in range(2):
                    dve.wait_ge(q["rstd"], b + 3)
                    dve.wait_ge(q["h"], b + 1)
                    own(dve.scalar_tensor_tensor(out=rp[:, b, 3:3 + T], in0=s.h[:, b, :], scalar=vecs[:, 0:1],
                                                 in1=w2[:, b, :], op0=ALU.mult, op1=ALU.mult))
                    own(dve.tensor_scalar(w1[:, b, :], rp[:, b, 0:T], vecs[:, 2:3], vecs[:, 1:2],
                                          ALU.mult, ALU.add))
                    for k in range(1, 4):
                        own(dve.scalar_tensor_tensor(out=w1[:, b, :], in0=rp[:, b, k:k + T],
                                                     scalar=vecs[:, 2 + k:3 + k], in1=w1[:, b, :],
                                                     op0=ALU.mult, op1=ALU.add))
                    dve.tensor_scalar(w2[:, b, :], w1[:, b, :], SIG_MIN, None, ALU.max).then_inc(q["conv"], 1)
                for b in range(2):
                    dve.wait_ge(q["sigmoid"], b + 1)
                    own(dve.tensor_tensor(s.conv[:, b, :], w1[:, b, :], w2[:, b, :], ALU.mult))


def recurrence(nc, s):
    a, T, ps = s.a, s.T, s.ps
    R = a["L0_attn_Wau"].shape[1]
    NG = T // G
    M = H // 2
    assert NG >= 3 and NC == 8 and H == 8 and C == 8 and G == 64 and R == 64
    with ExitStack() as c:
        def sb(name, shape):
            return sbuf(nc, c, name, shape)

        def full(name):
            return sb(name, [P, NC, H, C])

        w4 = sb("rc_w4", [P, 4, H * DK])
        wau = sb("rc_wau", [P, R])
        wad = sb("rc_wad", [R + 1, H * DK])
        wbeta = sb("rc_wbeta", [P, H])
        wbeta_rep = sb("rc_wbeta_rep", [P, H, DK])
        bsp = sb("rc_bsp", [P, H])
        asp = sb("rc_asp", [P, H])
        bbeta = sb("rc_bbeta", [P, H])
        norm_w = sb("rc_norm_w", [P, H])
        bau = sb("rc_bau", [R, 1])
        wo = sb("rc_wo", [P, M, D])
        xg = sb("rc_xg", [P, 2, G])
        xd = sb("rc_xd", [P, 2, G])
        sq = sb("rc_sq", [P, 2, 512])
        rn = sb("rc_rn", [P, 2, 512])
        qn, kn, dr, mp, spk, al, be, ex, ea, eb = (full(f"rc_{n}") for n in
                                                   "qn kn dr mp spk al be ex ea eb".split())
        au = sb("rc_au", [R, 2 * G])
        aus = sb("rc_aus", [R + 1, 2 * G])
        aux = sb("rc_aux", [R, 2 * G])
        neg_mem = sb("rc_neg_mem", [P, H])
        lg = sb("rc_lg", [P, NC * H])
        gm = sb("rc_gm", [P, NC * H])
        p8 = sb("rc_p8", [P, NC, H])
        qa, ka, kb, kab, kcb, kd, vb, t1 = (full(f"rc_{n}") for n in "qa ka kb kab kcb kd vb t1".split())
        wq = sb("rc_wq", [P, NC, H, 2, C])
        mt, mm, bt, imt, m2, p1, v1, tt, kcr, vbr, u0, ot = (
            sb(f"rc_{n}", [P, NC, 64]) for n in "mt mm bt imt m2 p1 v1 tt kcr vbr u0 ot".split())
        kdx = sb("rc_kdx", [P, NC, P])
        S = sb("rc_state", [P, H, DK])
        sd = sb("rc_state_decayed", [P, H, DK])
        ut = sb("rc_ut", [P, 64])
        ur = sb("rc_ur", [P, 64])
        ux = sb("rc_ux", [P, H, DK])
        q = signals(nc, c, "rc", "w_in ready xg xd drive_mm drive_in qkv_done au_done squared sums nq recip au_ready au_sig aus_ready "
                    "spikes weighed cnt_done alpha_mm beta_mm al_ready be_ready al_log be_sig ex_ready exps kq_ready kv_ready "
                    "m_mm m_ready m2_mm m2_ready p1_mm p1_ready v1_mm v1_ready tt_mm tt_ready rows_mm rows_ready "
                    "w_mm wq_ready xq_mm ut_ready ur_mm ur_ready ux_ready ds_mm bu_mm ot_ready s_ready "
                    "osq omean orms y_ready wo_mm y0_out y_out pe_turn dve_turn dve act")
        flat = lambda t: t[:].rearrange("p c h i -> p (c h i)")
        rows = lambda t: t[:].rearrange("p c h i -> p (c h) i")
        bank = lambda n: ps[:, n, :]
        bank_chi = lambda n: ps[:, n, :].rearrange("p (c h i) -> p c h i", c=NC, h=H)
        bank_ci = lambda n: ps[:, n, :].rearrange("p (c i) -> p c i", c=NC)
        per_head = lambda t: t[:].unsqueeze(1).unsqueeze(3).broadcast_to([P, NC, H, C])
        HALF = [slice(64 * b, 64 * b + 64) for b in range(2)]
        so = sb("rc_out_squares", [P, 512])
        ro = sb("rc_out_rms", [P, 512])
        yo = full("rc_out_normed")
        LOADS = 10 + 2 * 5
        pair = lambda t, m: t.rearrange("p c (b m) i -> p m b c i", b=2)[:, m]
        Q, K, V, DRV, AU, AL, SUM0, SUM1 = range(8)
        HH = H // 2
        DS = (V, AU)

        def groups(eng, group):
            group(0, True, False)
            with eng.Fori(1, NG - 1) as g:
                group(g, False, False)
            group(NG - 1, False, True)

        with nc.Block() as block:
            @block.sync
            def _(sp):
                for n, name in enumerate(("Wq", "Wk", "Wv", "Wspike")):
                    sp.dma_start(w4[:, n, :], a["L0_attn_" + name]).then_inc(q["w_in"], 16)
                sp.dma_start(wau[:], a["L0_attn_Wau"]).then_inc(q["w_in"], 16)
                sp.dma_start(wad[0:R, :], a["L0_attn_Wad"]).then_inc(q["w_in"], 16)
                sp.dma_start(wad[R:R + 1, :], a["L0_attn_bad"].unsqueeze(0)).then_inc(q["w_in"], 16)
                sp.dma_start(wbeta[:], a["L0_attn_Wbeta"]).then_inc(q["w_in"], 16)
                sp.dma_start(wo[:], a["L0_attn_Wo"].rearrange("(m r) n -> r m n", r=P)).then_inc(q["w_in"], 16)
                sp.dma_start(bau[:], a["L0_attn_bau"].unsqueeze(1)).then_inc(q["w_in"], 16)
                for b in range(2):
                    slots = slice(M * b, M * b + M)
                    sp.dma_start(bsp[:, slots], a["L0_attn_beta_spike"]).then_inc(q["w_in"], 16)
                    sp.dma_start(asp[:, slots], a["L0_attn_alpha_spike"]).then_inc(q["w_in"], 16)
                    sp.dma_start(norm_w[:, slots], a["L0_attn_head_norm_w"]).then_inc(q["w_in"], 16)
                    for e in range(2):
                        sp.dma_start(bbeta[HALF[e], slots],
                                     a["L0_attn_bbeta"][e:e + 1, :].broadcast_to([DK, M])).then_inc(q["w_in"], 16)

            @block.gpsimd
            def _(pool):
                for name in "beta_mm bu_mm".split():
                    pool.sem_inc(q[name], 1)
                def group(g, first, last):
                    pool.wait_ge(q["beta_mm"], g + 1)
                    pool.tensor_copy(xg[:], s.conv[:, :, bass.ds(g * G, G)]).then_inc(q["xg"], 1)
                    if not last:
                        pool.wait_ge(q["drive_mm"], g + 1)
                        pool.tensor_copy(xd[:], s.conv[:, :, bass.ds(g * G + G, G)]).then_inc(q["xd"], 1)

                pool.tensor_copy(xd[:], s.conv[:, :, 0:G]).then_inc(q["xd"], 1)
                groups(pool, group)

            @block.tensor
            def _(pe):
                def hold():
                    pe.sem_inc(q["pe_turn"], 1)

                def both(bank_n, lhs, rhs, width=64):
                    for n in range(NC):
                        for b in range(2):
                            ins = pe.matmul(ps[HALF[b], bank_n, 64 * n:64 * n + width], lhs(n, b), rhs(n, b),
                                            start=True, stop=True)
                    return ins

                chunk = lambda t: (lambda n, b: t[HALF[b], n].rearrange("p h i -> p (h i)"))
                mat = lambda t: (lambda n, b: t[HALF[b], n, :])
                eye = lambda n, b: s.ident[HALF[b], HALF[b]]

                def project(weights, bank_n, x):
                    for m in range(M):
                        ins = pe.matmul(pair(bank_chi(bank_n), m), weights[:, P * m:P * m + P], x,
                                        start=True, stop=True)
                    return ins

                def output_mean(g):
                    pe.wait_ge(q["osq"], g + 1)
                    pe.matmul(bank(AL), s.ones_block, so[:], start=True, stop=True).then_inc(q["omean"], 1)

                def project_output(g):
                    pe.wait_ge(q["y_ready"], g + 1)
                    hold()
                    for m in range(M):
                        ins = pe.matmul(ps[:, AL, 0:2 * G], wo[:, m, :], pair(yo[:], m), start=(m == 0),
                                        stop=(m == M - 1))
                    ins.then_inc(q["wo_mm"], 1)

                def group(g, first, last):
                    pe.wait_ge(q["xg"], g + 1)
                    pe.wait_ge(q["s_ready"], 2 * g * NC + 2)
                    if not first:
                        output_mean(g - 1)
                    hold()
                    for n in range(3):
                        project(w4[:, n, :], n, xg[:]).then_inc(q["qkv_done"], 1)
                    pe.wait_ge(q["drive_in"], g + 1)
                    pe.matmul(ps[0:R, AU, 0:2 * G], wau[:], xg[:].rearrange("p b t -> p (b t)"),
                              start=True, stop=True).then_inc(q["au_done"], 1)
                    if not first:
                        project_output(g - 1)
                    pe.wait_ge(q["weighed"], g + 1)
                    pe.matmul(bank(DRV), s.ones_block, flat(t1), start=True, stop=False, skip_group_check=True)
                    for m in range(M):
                        ins = pe.matmul(pair(bank_chi(DRV), m),
                                        wbeta_rep[:, 2 * m:2 * m + 2, :].rearrange("p h d -> p (h d)"), xg[:],
                                        start=False, stop=(m == M - 1), skip_group_check=True)
                    ins.then_inc(q["beta_mm"], 1)
                    for n in range(2):
                        pe.wait_ge(q["squared"], 2 * g + n + 1)
                        pe.matmul(bank(SUM0 + n), s.ones_block, sq[:, n, :], start=True, stop=True)\
                          .then_inc(q["sums"], 1)
                    pe.wait_ge(q["au_ready"], g + 1)
                    pe.wait_ge(q["spikes"], g + 1)
                    pe.matmul(bank(AU), s.ones_block, flat(spk), start=True, stop=True).then_inc(q["cnt_done"], 1)
                    pe.wait_ge(q["aus_ready"], g + 1)
                    if not first:
                        pe.wait_ge(q["y_out"], g)
                    hold()
                    project(wad[:], AL, aus[:]).then_inc(q["alpha_mm"], 1)
                    pe.wait_ge(q["kq_ready"], g + 1)
                    hold()
                    both(Q, chunk(kb), chunk(kab)).then_inc(q["m_mm"], 1)
                    both(K, chunk(kab), chunk(kb)).then_inc(q["m_mm"], 1)
                    both(DRV, chunk(kb), chunk(qa)).then_inc(q["m_mm"], 1)
                    pe.wait_ge(q["kv_ready"], g + 1)
                    hold()
                    both(V, chunk(vb), eye).then_inc(q["rows_mm"], 1)
                    pe.wait_ge(q["m_ready"], g + 1)
                    hold()
                    both(Q, mat(mt), mat(mm)).then_inc(q["m2_mm"], 1)
                    both(AL, chunk(kcb), eye).then_inc(q["rows_mm"], 1)
                    pe.wait_ge(q["m2_ready"], g + 1)
                    hold()
                    both(DRV, mat(m2), mat(imt)).then_inc(q["p1_mm"], 1)
                    both(SUM1, chunk(kd), eye).then_inc(q["rows_mm"], 1)
                    pe.wait_ge(q["p1_ready"], g + 1)
                    hold()
                    both(K, mat(m2), mat(p1)).then_inc(q["v1_mm"], 1)
                    if not last:
                        pe.wait_ge(q["xd"], g + 2)
                        hold()
                        project(w4[:, 3, :], DRV, xd[:]).then_inc(q["drive_mm"], 1)
                    pe.wait_ge(q["v1_ready"], g + 1)
                    hold()
                    both(Q, mat(m2), mat(v1)).then_inc(q["tt_mm"], 1)
                    pe.wait_ge(q["tt_ready"], g + 1)
                    pe.wait_ge(q["rows_ready"], 4 * g + 4)
                    hold()
                    both(SUM0, mat(kcr), mat(tt)).then_inc(q["w_mm"], 1)
                    both(SUM1, mat(vbr), mat(tt)).then_inc(q["w_mm"], 1)
                    pe.wait_ge(q["wq_ready"], 2 * g + 1)
                    for n in range(NC):
                        xq = ps[:, 3 * (n % 2), 0:2 * 64].rearrange("p (h k i) -> p h k i", h=H, k=2)
                        if n >= 2:
                            pe.wait_ge(q["ot_ready"], g * NC + n - 1)
                        for h in range(H):
                            if h % HH == 0:
                                pe.wait_ge(q["s_ready"], 2 * (g * NC + n) + h // HH + 1)
                                hold()
                            for b in range(2):
                                ins = pe.matmul(xq[HALF[b], h, :, :], S[HALF[b], h, :], wq[HALF[b], n, h, :, :],
                                                start=(h == 0), stop=False, skip_group_check=True)
                        ins.then_inc(q["xq_mm"], 1)
                        pe.wait_ge(q["ut_ready"], g * NC + n + 1)
                        hold()
                        for k in (K, AL):
                            for b in range(2):
                                ins = pe.matmul(ps[HALF[b], k, 0:64], ut[HALF[b], :], eye(n, b),
                                                start=True, stop=True)
                            ins.then_inc(q["ur_mm"], 1)
                        for k in range(2):
                            pe.wait_ge(q["ux_ready"], 2 * (g * NC + n) + k + 1)
                            pe.matmul(ps[:, DS[k], 0:HH * DK], kdx[:, n, :],
                                      ux[:, HH * k:HH * k + HH, :].rearrange("p h v -> p (h v)"),
                                      start=True, stop=True).then_inc(q["ds_mm"], 1)
                        pe.wait_ge(q["ur_ready"], g * NC + n + 1)
                        hold()
                        for b in range(2):
                            ins = pe.matmul(xq[HALF[b], :, 1, :], ur[HALF[b], :], bt[HALF[b], n, :],
                                            start=False, stop=True, skip_group_check=True)
                        ins.then_inc(q["bu_mm"], 1)
                    if last:
                        output_mean(g)
                        project_output(g)

                pe.wait_ge(q["w_in"], LOADS * 16)
                pe.wait_ge(q["ready"], 1)
                pe.wait_ge(q["xd"], 1)
                hold()
                project(w4[:, 3, :], DRV, xd[:]).then_inc(q["drive_mm"], 1)
                groups(pe, group)

            @block.scalar
            def _(act):
                def sigmoid_log(t):
                    own(act.activation(t, t, ACT.Exp, scale=-1.0))
                    return act.activation(t, t, ACT.Ln, bias=1.0)

                def output_rms(g):
                    act.wait_ge(q["omean"], g + 1)
                    own(act.activation(ro[:], bank(AL), ACT.Ln, scale=1.0 / DK, bias=1e-6))
                    act.activation(ro[:], ro[:], ACT.Exp, scale=-0.5).then_inc(q["orms"], 1)

                def store_output(g):
                    act.wait_ge(q["wo_mm"], g + 1)
                    act.activation(s.y[:, 0, bass.ds(g * G, G)], ps[:, AL, 0:G], ACT.Copy).then_inc(q["y0_out"], 1)
                    act.activation(s.y[:, 1, bass.ds(g * G, G)], ps[:, AL, G:2 * G], ACT.Copy).then_inc(q["y_out"], 1)

                own = Link(act, q["act"])
                def group(g, first, last):
                    own.restart()
                    if not first:
                        output_rms(g - 1)
                    for n in range(2):
                        act.wait_ge(q["qkv_done"], 3 * g + n + 1)
                        act.activation(sq[:, n, :], bank(n), ACT.Square).then_inc(q["squared"], 1)
                    act.wait_ge(q["au_ready"], g + 1)
                    own(sigmoid_log(aux[:]))
                    act.activation(aux[:], aux[:], ACT.Exp, scale=-1.0).then_inc(q["au_sig"], 1)
                    if not first:
                        store_output(g - 1)
                    act.wait_ge(q["be_ready"], g + 1)
                    own(sigmoid_log(flat(be)))
                    act.activation(flat(be), flat(be), ACT.Exp, scale=-1.0).then_inc(q["be_sig"], 1)
                    act.wait_ge(q["al_ready"], g + 1)
                    sigmoid_log(flat(al)).then_inc(q["al_log"], 1)
                    act.wait_ge(q["nq"], g + 1)
                    own(act.activation(rn[:], rn[:], ACT.Ln))
                    own(act.activation(rn[:], rn[:], ACT.Exp, scale=0.5))
                    own(act.activation(rn[:], rn[:], ACT.Ln, bias=1e-6))
                    act.activation(rn[:], rn[:], ACT.Exp, scale=-1.0).then_inc(q["recip"], 1)
                    act.wait_ge(q["ex_ready"], g + 1)
                    own(act.activation(flat(ea), flat(ex), ACT.Exp, scale=-1.0))
                    own(act.activation(flat(eb), flat(ex), ACT.Exp))
                    own(act.activation(gm[:], lg[:], ACT.Exp))
                    act.activation(p8[:].rearrange("p c h -> p (c h)"), p8[:].rearrange("p c h -> p (c h)"),
                                   ACT.Exp).then_inc(q["exps"], 1)
                    act.wait_ge(q["rows_mm"], 3 * g + 1)
                    act.activation(vbr[:], bank_ci(V), ACT.Copy).then_inc(q["rows_ready"], 1)
                    act.wait_ge(q["m2_mm"], g + 1)
                    act.activation(m2[:], bank_ci(Q), ACT.Copy).then_inc(q["m2_ready"], 1)
                    act.wait_ge(q["rows_mm"], 3 * g + 2)
                    act.activation(kcr[:], bank_ci(AL), ACT.Copy).then_inc(q["rows_ready"], 1)
                    act.wait_ge(q["rows_mm"], 3 * g + 3)
                    act.activation(kdx[HALF[0], :, HALF[0]], bank_ci(SUM1)[HALF[0]], ACT.Copy)\
                       .then_inc(q["rows_ready"], 1)
                    act.activation(kdx[HALF[1], :, HALF[1]], bank_ci(SUM1)[HALF[1]], ACT.Copy)\
                       .then_inc(q["rows_ready"], 1)
                    act.wait_ge(q["v1_mm"], g + 1)
                    act.activation(v1[:], bank_ci(K), ACT.Copy).then_inc(q["v1_ready"], 1)
                    act.wait_ge(q["w_mm"], 2 * g + 1)
                    act.activation(wq[:, :, :, 0, :].rearrange("p c h i -> p (c h) i"),
                                   bank(SUM0).rearrange("p (n i) -> p n i", i=C), ACT.Copy)\
                       .then_inc(q["wq_ready"], 1)
                    act.wait_ge(q["w_mm"], 2 * g + 2)
                    act.activation(u0[:], bank_ci(SUM1), ACT.Copy).then_inc(q["wq_ready"], 1)
                    for n in range(NC):
                        xq = ps[:, 3 * (n % 2), 0:2 * 64].rearrange("p (h k i) -> p h k i", h=H, k=2)
                        act.wait_ge(q["ur_mm"], 2 * (g * NC + n) + 2)
                        if n == 0:
                            act.wait_ge(q["bu_mm"], g * NC + 1)
                        else:
                            act.wait_ge(q["bu_mm"], g * NC + n + 1)
                        act.activation(ur[:], ps[:, AL, 0:64], ACT.Copy).then_inc(q["ur_ready"], 1)
                        act.wait_ge(q["bu_mm"], g * NC + n + 2)
                        act.activation(ot[:, n, :].rearrange("p (h i) -> p h i", h=H), xq[:, :, 1, :], ACT.Copy)\
                           .then_inc(q["ot_ready"], 1)
                    act.wait_ge(q["ot_ready"], g * NC + NC)
                    act.activation(so[:], ot[:].rearrange("p c i -> p (c i)"), ACT.Square).then_inc(q["osq"], 1)
                    if last:
                        output_rms(g)
                        store_output(g)

                groups(act, group)

            @block.vector
            def _(dve):
                own = Link(dve, q["dve"])
                own(dve.memset(neg_mem[:], 0.0))
                own(dve.memset(aus[:], 1.0))
                own(dve.memset(ex[:], 0.0))
                for t in (mt, mm, bt, kdx):
                    own(dve.memset(t[:], 0.0))
                for k in range(2):
                    dve.memset(S[:, HH * k:HH * k + HH, :], 0.0).then_inc(q["s_ready"], 1)
                dve.wait_ge(q["w_in"], LOADS * 16)
                dve.tensor_copy(wbeta_rep[:], wbeta[:].unsqueeze(2).broadcast_to([P, H, DK])).then_inc(q["ready"], 1)
                dve.wait_ge(q["ready"], 1)
                dve.wait_ge(q["s_ready"], 2)
                exr, alr = rows(ex), rows(al)

                def norm_output(g):
                    dve.wait_ge(q["orms"], g + 1)
                    own(dve.tensor_tensor(flat(yo), ot[:].rearrange("p c i -> p (c i)"), ro[:], ALU.mult))
                    dve.tensor_tensor(yo[:], yo[:], per_head(norm_w), ALU.mult).then_inc(q["y_ready"], 1)

                def read_drive(count):
                    dve.wait_ge(q["drive_mm"], count)
                    dve.tensor_scalar(flat(dr), bank(DRV), 1.0 / THR, None, ALU.mult).then_inc(q["drive_in"], 1)
                    dve.wait_ge(q["drive_in"], count)

                def membranes(n, steps):
                    for i in steps:
                        own(dve.scalar_tensor_tensor(out=mp[:, n, :, i], in0=neg_mem[:], scalar=-DECAY,
                                                     in1=dr[:, n, :, i], op0=ALU.mult, op1=ALU.add))
                        own(dve.scalar_tensor_tensor(out=neg_mem[:], in0=mp[:, n, :, i], scalar=1.0,
                                                     in1=mp[:, n, :, i], op0=ALU.is_gt, op1=ALU.subtract))

                def group(g, first, last):
                    own.restart()
                    dve.tensor_scalar(flat(spk), flat(mp), 1.0, None, ALU.is_gt).then_inc(q["spikes"], 1)
                    dve.wait_ge(q["spikes"], g + 1)
                    dve.tensor_tensor(t1[:], spk[:], per_head(bsp), ALU.mult).then_inc(q["weighed"], 1)
                    own(dve.tensor_tensor(al[:], spk[:], per_head(asp), ALU.mult))
                    if not first:
                        norm_output(g - 1)
                    dve.wait_ge(q["au_done"], g + 1)
                    own(dve.tensor_scalar(au[:], ps[0:R, AU, 0:2 * G], bau[:, 0:1], None, ALU.add))
                    dve.tensor_scalar(aux[:], au[:], SIG_MIN, None, ALU.max).then_inc(q["au_ready"], 1)
                    dve.wait_ge(q["beta_mm"], g + 2)
                    own(dve.tensor_tensor(be[:], bank_chi(DRV), per_head(bbeta), ALU.add))
                    dve.tensor_scalar(flat(be), flat(be), SIG_MIN, None, ALU.max).then_inc(q["be_ready"], 1)
                    dve.wait_ge(q["au_sig"], g + 1)
                    dve.tensor_tensor(aus[0:R, :], au[:], aux[:], ALU.mult).then_inc(q["aus_ready"], 1)
                    dve.wait_ge(q["sums"], 2 * g + 2)
                    dve.tensor_scalar(rn[:].rearrange("p a n -> p (a n)"),
                                      ps[:, SUM0:SUM0 + 2, :].rearrange("p a n -> p (a n)"), TINY, None, ALU.max)\
                       .then_inc(q["nq"], 1)
                    dve.wait_ge(q["alpha_mm"], g + 1)
                    own(dve.tensor_tensor(flat(al), flat(al), bank(AL), ALU.add))
                    dve.tensor_scalar(flat(al), flat(al), SIG_MIN, None, ALU.max).then_inc(q["al_ready"], 1)
                    if not first:
                        dve.wait_ge(q["wo_mm"], g)
                    dve.wait_ge(q["cnt_done"], g + 1)
                    dve.wait_ge(q["beta_mm"], g + 2)
                    own(dve.tensor_scalar(flat(t1), bank(AU), 0.5, None, ALU.is_gt))
                    dve.wait_ge(q["al_log"], g + 1)
                    own(dve.scalar_tensor_tensor(out=flat(al), in0=flat(al), scalar=LOG_DECAY_MAX, in1=flat(t1),
                                                 op0=ALU.min, op1=ALU.mult))
                    own(dve.tensor_scalar(exr[:, :, 2], alr[:, :, 3], -1.0, None, ALU.mult))
                    for i in (1, 0):
                        own(dve.tensor_tensor(exr[:, :, i], exr[:, :, i + 1], alr[:, :, i + 1], ALU.subtract))
                    own(dve.tensor_tensor(lg[:], exr[:, :, 0], alr[:, :, 0], ALU.subtract))
                    own(dve.tensor_copy(exr[:, :, 4], alr[:, :, 4]))
                    for i in (5, 6, 7):
                        own(dve.tensor_tensor(exr[:, :, i], exr[:, :, i - 1], alr[:, :, i], ALU.add))
                    dve.tensor_tensor(p8[:].rearrange("p c h -> p (c h)"), lg[:], exr[:, :, 7], ALU.subtract)\
                       .then_inc(q["ex_ready"], 1)
                    dve.wait_ge(q["be_sig"], g + 1)
                    own(dve.tensor_tensor(flat(be), flat(be), flat(t1), ALU.mult))
                    dve.wait_ge(q["qkv_done"], 3 * g + 3)
                    dve.wait_ge(q["recip"], g + 1)
                    own(dve.tensor_tensor(flat(qn), bank(Q), rn[:, 0, :], ALU.mult))
                    own(dve.tensor_tensor(flat(kn), bank(K), rn[:, 1, :], ALU.mult))
                    dve.wait_ge(q["exps"], g + 1)
                    own(dve.tensor_tensor(flat(qa), flat(qn), flat(ea), ALU.mult))
                    own(dve.tensor_tensor(flat(ka), flat(kn), flat(ea), ALU.mult))
                    own(dve.tensor_tensor(flat(kb), flat(kn), flat(eb), ALU.mult))
                    dve.scalar_tensor_tensor(out=flat(kab), in0=flat(ka), scalar=-1.0, in1=flat(be),
                                             op0=ALU.mult, op1=ALU.mult).then_inc(q["kq_ready"], 1)
                    dve.wait_ge(q["kq_ready"], g + 1)
                    own(dve.tensor_tensor(flat(vb), bank(V), flat(be), ALU.mult))
                    gmb = gm[:].unsqueeze(2).broadcast_to([P, NC * H, C])
                    own(dve.tensor_tensor(rows(kcb), rows(kab), gmb, ALU.mult))
                    own(dve.tensor_tensor(wq[:, :, :, 1, :].rearrange("p c h i -> p (c h) i"), rows(qa), gmb,
                                          ALU.mult))
                    dve.tensor_tensor(rows(kd), rows(kb), rows(ea)[:, :, 7:8].broadcast_to([P, NC * H, C]),
                                      ALU.mult).then_inc(q["kv_ready"], 1)
                    for k, (t, n, mask) in enumerate(((mt, Q, s.rows_first), (mm, K, s.rows_last),
                                                      (bt, DRV, s.rows_to))):
                        dve.wait_ge(q["m_mm"], 3 * g + k + 1)
                        dve.sem_inc(q["dve_turn"], 1)
                        own(dve.copy_predicated(t[:], mask.bitcast(U32).unsqueeze(1).broadcast_to([P, NC, 64]),
                                                bank_ci(n)))
                    dve.tensor_tensor(imt[:], mt[:], s.ident64.unsqueeze(1).broadcast_to([P, NC, 64]), ALU.add)\
                       .then_inc(q["m_ready"], 1)
                    dve.wait_ge(q["p1_mm"], g + 1)
                    dve.wait_ge(q["m_ready"], g + 1)
                    dve.tensor_tensor(p1[:], bank_ci(DRV), imt[:], ALU.add).then_inc(q["p1_ready"], 1)
                    dve.wait_ge(q["tt_mm"], g + 1)
                    dve.wait_ge(q["p1_ready"], g + 1)
                    dve.tensor_tensor(tt[:], bank_ci(Q), p1[:], ALU.add).then_inc(q["tt_ready"], 1)
                    dve.wait_ge(q["wq_ready"], 2 * g + 2)
                    if not last:
                        read_drive(g + 2)
                    for n in range(NC):
                        xq = ps[:, 3 * (n % 2), 0:2 * 64].rearrange("p (h k i) -> p h k i", h=H, k=2)
                        dve.wait_ge(q["xq_mm"], g * NC + n + 1)
                        dve.tensor_tensor(ut[:].rearrange("p (h i) -> p h i", h=H), xq[:, :, 0, :],
                                          u0[:, n, :].rearrange("p (h i) -> p h i", h=H), ALU.add)\
                           .then_inc(q["ut_ready"], 1)
                        own(dve.tensor_tensor(sd[:], S[:], p8[:, n, :].unsqueeze(2).broadcast_to([P, H, DK]),
                                              ALU.mult))
                        dve.wait_ge(q["ur_mm"], 2 * (g * NC + n) + 1)
                        for k in range(2):
                            dve.tensor_tensor(ux[:, HH * k:HH * k + HH, :],
                                              ps[:, K, 0:64].unsqueeze(1).broadcast_to([P, HH, DK]),
                                              s.head_mask[:, HH * k:HH * k + HH].unsqueeze(2)
                                              .broadcast_to([P, HH, DK]), ALU.mult).then_inc(q["ux_ready"], 1)
                        if not last:
                            membranes(n, range(0, 2))
                        for k in range(2):
                            dve.wait_ge(q["ds_mm"], 2 * (g * NC + n) + k + 1)
                            dve.tensor_tensor(S[:, HH * k:HH * k + HH, :], sd[:, HH * k:HH * k + HH, :],
                                              ps[:, DS[k], 0:HH * DK].rearrange("p (h v) -> p h v", v=DK),
                                              ALU.add).then_inc(q["s_ready"], 1)
                        if not last:
                            membranes(n, range(2, C))
                        dve.wait_ge(q["s_ready"], 2 * (g * NC + n) + 4)
                    if last:
                        norm_output(g)
                        dve.wait_ge(q["wo_mm"], g + 1)

                read_drive(1)
                for n in range(NC):
                    membranes(n, range(C))
                groups(dve, group)

def gate_and_ff(nc, s):
    a, T, NB, BL, ps, mod = s.a, s.T, s.NB, s.BL, s.ps, s.mod
    R = a["L0_attn_Wu1"].shape[1]
    FF = a["L0_attn_Wff1"].shape[1]
    FK = FF // P
    NU = 2 * NB
    with ExitStack() as c:
        w1 = sbuf(nc, c, "gf_values", [P, 2, T])
        w2 = sbuf(nc, c, "gf_factors", [P, 2, T])
        wu1 = sbuf(nc, c, "gf_wu1", [P, R])
        wu2 = sbuf(nc, c, "gf_wu2", [R, P])
        vecs = sbuf(nc, c, "gf_vectors", [P, 3])
        wff = sbuf(nc, c, "gf_wff13", [P, 2, FF])
        wff2 = sbuf(nc, c, "gf_wff2", [P, FK, P])
        act1 = sbuf(nc, c, "gf_act", [P, FK, BL])
        up = sbuf(nc, c, "gf_up", [P, FK, BL])
        q = signals(nc, c, "gf", "w_in mm pre sig u_ready y_ready squares rms z_ready ff_mm ff_pre ff_sig ff_ready "
                                 "ff_out x_ready sums centered squares2 rstd dve act")
        banks = halves(s)
        blk = lambda t, b: t[:, b, :].rearrange("p (n l) -> p n l", l=BL)
        f_a = ps[:, 0:FK, 0:BL]
        f_b = ps[:, FK:2 * FK, 0:BL]
        assert FK == 4
        with nc.Block() as block:
            @block.sync
            def _(sp):
                for dst, src in ((wu1[:], a["L0_attn_Wu1"]), (wu2[:], a["L0_attn_Wu2"]),
                                 (vecs[0:R, 0:1], a["L0_attn_bu1"].unsqueeze(1)),
                                 (vecs[:, 1:2], a["L0_attn_bu2"].unsqueeze(1)),
                                 (vecs[:, 2:3], a["L0_attn_ff_norm_w"].unsqueeze(1)),
                                 (wff[:, 0, :], a["L0_attn_Wff1"]), (wff[:, 1, :], a["L0_attn_Wff3"]),
                                 (wff2[:], a["L0_attn_Wff2"].rearrange("(k p) n -> p k n", p=P))):
                    sp.dma_start(dst, src).then_inc(q["w_in"], 16)

            @block.tensor
            def _(pe):
                def over(b, lhs, src, rows=P):
                    for n in range(NB):
                        ins = pe.matmul(ps[0:rows, 4 * b + n, 0:BL], lhs, src[0:lhs.shape[0], b, BL * n:BL * n + BL],
                                        start=True, stop=True)
                    return ins

                pe.wait_ge(q["w_in"], 8 * 16)
                for b in range(2):
                    over(b, wu1[:], s.h, R).then_inc(q["mm"], 1)
                for b in range(2):
                    pe.wait_ge(q["u_ready"], b + 1)
                    over(b, wu2[:], w1).then_inc(q["mm"], 1)
                for b in range(2):
                    pe.wait_ge(q["squares"], b + 1)
                    over(b, s.ones[:], w2).then_inc(q["mm"], 1)
                for u in range(NU):
                    b, n = divmod(u, NB)
                    pe.wait_ge(q["z_ready"], b + 1)
                    pe.wait_ge(q["z_ready"], 2)
                    if u:
                        pe.wait_ge(q["ff_out"], u)
                    for m in range(2):
                        for k in range(FK):
                            ins = pe.matmul(ps[:, FK * m + k, 0:BL], wff[:, m, P * k:P * k + P],
                                            w2[:, b, BL * n:BL * n + BL], start=True, stop=True)
                    ins.then_inc(q["ff_mm"], 1)
                    pe.wait_ge(q["ff_ready"], u + 1)
                    for k in range(FK):
                        ins = pe.matmul(ps[:, 0, 0:BL], wff2[:, k, :], up[:, k, :], start=(k == 0),
                                        stop=(k == FK - 1))
                    ins.then_inc(q["ff_mm"], 1)
                for b in range(2):
                    pe.wait_ge(q["x_ready"], 2)
                    over(b, s.ones[:], s.x).then_inc(q["sums"], 1)
                for b in range(2):
                    pe.wait_ge(q["squares2"], b + 1)
                    over(b, s.ones[:], w2).then_inc(q["sums"], 1)

            @block.scalar
            def _(act):
                own = Link(act, q["act"])

                def sigmoid(t):
                    own(act.activation(t, t, ACT.Exp, scale=-1.0))
                    own(act.activation(t, t, ACT.Ln, bias=1.0))
                    return act.activation(t, t, ACT.Exp, scale=-1.0)

                for b in range(2):
                    act.wait_ge(q["pre"], b + 1)
                    sigmoid(w2[0:R, b, :]).then_inc(q["sig"], 1)
                for b in range(2):
                    act.wait_ge(q["pre"], b + 3)
                    sigmoid(w2[:, b, :]).then_inc(q["sig"], 1)
                for b in range(2):
                    act.wait_ge(q["y_ready"], b + 1)
                    act.activation(w2[:, b, :], w1[:, b, :], ACT.Square).then_inc(q["squares"], 1)
                for b in range(2):
                    act.wait_ge(q["mm"], b + 5)
                    own(act.activation(blk(w2, b), banks[b], ACT.Ln, scale=1.0 / D, bias=1e-6))
                    act.activation(w2[:, b, :], w2[:, b, :], ACT.Exp, scale=-0.5).then_inc(q["rms"], 1)
                for u in range(NU):
                    act.wait_ge(q["ff_pre"], u + 1)
                    sigmoid(act1[:]).then_inc(q["ff_sig"], 1)
                for b in range(2):
                    act.wait_ge(q["centered"], b + 1)
                    act.activation(w2[:, b, :], w1[:, b, :], ACT.Square).then_inc(q["squares2"], 1)
                for b in range(2):
                    act.wait_ge(q["sums"], b + 3)
                    own(act.activation(blk(w2, b), banks[b], ACT.Ln, scale=1.0 / D, bias=1e-5))
                    act.activation(w2[:, b, :], w2[:, b, :], ACT.Exp, scale=-0.5).then_inc(q["rstd"], 1)

            @block.vector
            def _(dve):
                own = Link(dve, q["dve"])
                dve.wait_ge(q["w_in"], 8 * 16)
                for b in range(2):
                    dve.wait_ge(q["mm"], b + 1)
                    own(dve.tensor_scalar(blk(w1, b)[0:R], banks[b][0:R], vecs[0:R, 0:1], None, ALU.add))
                    dve.tensor_scalar(w2[0:R, b, :], w1[0:R, b, :], SIG_MIN, None, ALU.max).then_inc(q["pre"], 1)
                for b in range(2):
                    dve.wait_ge(q["sig"], b + 1)
                    dve.tensor_tensor(w1[0:R, b, :], w1[0:R, b, :], w2[0:R, b, :], ALU.mult).then_inc(q["u_ready"], 1)
                for b in range(2):
                    dve.wait_ge(q["mm"], b + 3)
                    dve.tensor_scalar(blk(w2, b), banks[b], vecs[:, 1:2], SIG_MIN, ALU.add, ALU.max)\
                       .then_inc(q["pre"], 1)
                for b in range(2):
                    dve.wait_ge(q["sig"], b + 3)
                    own(dve.tensor_tensor(w1[:, b, :], s.y[:, b, :], w2[:, b, :], ALU.mult))
                    dve.tensor_tensor(w1[:, b, :], w1[:, b, :], s.h[:, b, :], ALU.add).then_inc(q["y_ready"], 1)
                for b in range(2):
                    dve.wait_ge(q["rms"], b + 1)
                    dve.wait_ge(q["y_ready"], b + 1)
                    dve.scalar_tensor_tensor(out=w2[:, b, :], in0=w1[:, b, :], scalar=vecs[:, 2:3],
                                             in1=w2[:, b, :], op0=ALU.mult, op1=ALU.mult).then_inc(q["z_ready"], 1)
                for u in range(NU):
                    b, n = divmod(u, NB)
                    dve.wait_ge(q["ff_mm"], 2 * u + 1)
                    dve.tensor_scalar(act1[:], f_a, SIG_MIN, None, ALU.max).then_inc(q["ff_pre"], 1)
                    own(dve.tensor_copy(up[:], f_b))
                    own(dve.tensor_tensor(up[:], up[:], f_a, ALU.mult))
                    dve.wait_ge(q["ff_sig"], u + 1)
                    dve.tensor_tensor(up[:], up[:], act1[:], ALU.mult).then_inc(q["ff_ready"], 1)
                    dve.wait_ge(q["ff_mm"], 2 * u + 2)
                    dve.tensor_tensor(w1[:, b, BL * n:BL * n + BL], w1[:, b, BL * n:BL * n + BL],
                                      ps[:, 0, 0:BL], ALU.add).then_inc(q["ff_out"], 1)
                dve.wait_ge(q["ff_out"], NU)
                for b in range(2):
                    dve.scalar_tensor_tensor(out=s.x[:, b, :], in0=w1[:, b, :], scalar=mod[:, GATE_A, b:b + 1],
                                             in1=s.x[:, b, :], op0=ALU.mult, op1=ALU.add).then_inc(q["x_ready"], 1)
                dve.wait_ge(q["x_ready"], 2)
                for b in range(2):
                    dve.wait_ge(q["sums"], b + 1)
                    dve.scalar_tensor_tensor(out=blk(w1, b), in0=banks[b], scalar=-1.0 / D, in1=blk(s.x, b),
                                             op0=ALU.mult, op1=ALU.add).then_inc(q["centered"], 1)
                for b in range(2):
                    dve.wait_ge(q["rstd"], b + 1)
                    dve.wait_ge(q["centered"], b + 1)
                    own(dve.tensor_tensor(w1[:, b, :], w1[:, b, :], w2[:, b, :], ALU.mult))
                    own(dve.tensor_scalar(s.xa[:, XPAD + T * b:XPAD + T * b + T], w1[:, b, :],
                                          mod[:, SC_B, b:b + 1], mod[:, SH_B, b:b + 1], ALU.mult, ALU.add))
                own(dve.memset(s.xa[:, 0:XPAD], 0.0))



def windowed_layers(nc, s, out):
    a, T, NB, BL, ps, mod, xa = s.a, s.T, s.NB, s.BL, s.ps, s.mod, s.xa
    DEPTH = a["wqkv"].shape[0]
    INNER = HEADS * DH
    FI = a["w1"].shape[2] // 2
    NT = 2 * T // TILE
    NU = 2 * NB
    CH = [min(P, FI - P * k) for k in range((FI + P - 1) // P)]
    NCH = len(CH)
    NS = NCH * NU
    assert NCH == 3
    with ExitStack() as c:
        def sb(name, shape):
            return sbuf(nc, c, name, shape)

        xb = sb("xb", [P, XPAD + 2 * T])
        fs = sb("ff_values", [P, 2, T])
        fq = sb("ff_factors", [P, 2, T])
        tabs = sb("rotary_tables", [P, NT, 4 * DH])
        masks = sb("masks", [P, NT, 2 * WIN])
        cols = sb("tile_columns", [P, NT + 1])
        wqkv = sb("wqkv", [P, 3 * INNER])
        wo = sb("wo_pairs", [P, PAIRS, D])
        scales = sb("qk_scales", [P, 4 * DH])
        w1 = sb("w1", [P, 2 * FI])
        w2 = sb("w2", [P, NCH, D])
        vecs = sb("layer_vectors", [P, 9])
        xs = sb("xs", [P, HALO + TILE])
        xr = sb("xr", [P, 2, TILE])
        tab = sb("tab", [P, 4 * DH])
        mask = sb("mask", [P, 2 * WIN])
        sq = fs[:].rearrange("p b t -> p (b t)")[:, 0:2 * INNER] if T >= INNER else sb("sq", [P, 2 * INNER])[:]
        t3 = fq[:].rearrange("p b t -> p (b t)")[:, 0:INNER] if 2 * T >= INNER else sb("t3", [P, INNER])[:]
        rn = sb("rn", [P, 2 * HEADS])
        qr = sb("qr", [P, INNER])
        kr = sb("kr", [P, INNER])
        t2 = sb("t2", [P, INNER])
        qt = sb("qt", [P, PAIRS, TILE])
        kt = sb("kt", [P, PAIRS, HALO + TILE])
        vs = sb("vs", [P, 4, PAIRS * DH])
        s1 = sb("s1", [P, 2, PAIRS, 2 * WIN])
        mx = sb("mx", [P, 2, PAIRS])
        pr = sb("pr", [P, PAIRS, 2, 2 * WIN])
        rs = sb("rs", [P, 2 * PAIRS])
        pt = sb("pt", [P, PAIRS, TILE])
        ot = sb("ot", [P, PAIRS, TILE])
        gel = sb("gel", [P, 3, BL])
        hid = sb("hid", [P, 3, BL])
        q = signals(nc, c, "wl", "tabs_in attn_w_in ff_w_in cleared xs tab mask sim qk pt_mm o_mm v_mm q_t k_t wo_mm exp "
                                 "squares rnorm pt_in o_in v_in qk_in smax p_ready ssq q_parts q_added rotq rotk xb_ready "
                                 "fs_ready ln_sums centered squares2 rstd xn_ready w1_mm gelu hid_ready w2_mm "
                                 "xa_ready pe_turn dve_turn pool_turn dve act pool last out_done")
        blk = lambda t, b: t[:, b, :].rearrange("p (n l) -> p n l", l=BL)
        banks = halves(s)
        two = lambda n: ps[:, n:n + 2, :]
        Q0, K0, S0, O0 = 0, 2, 4, 6
        V0 = (S0, O0)
        heads = lambda t: t.rearrange("p (h d) -> p h d", d=DH)

        def tiles(eng, base, body):
            body(None, base, -1)
            with eng.Fori(0, NT - 1) as t:
                body(base + t, base + t + 1, t)
            body(base + (NT - 1), None, NT - 1)

        with nc.Block() as block:
            @block.sync
            def _(sp):
                sp.dma_start(tabs[:], s.const["tabs"]).then_inc(q["tabs_in"], 16)
                sp.dma_start(masks[:], s.const["masks"]).then_inc(q["tabs_in"], 16)
                sp.dma_start(cols[:], s.const["cols"]).then_inc(q["tabs_in"], 16)
                with sp.Fori(0, DEPTH) as l:
                    sp.wait_ge(q["wo_mm"], l * NT + 1)
                    sp.wait_ge(q["tab"], l * NT + 1)
                    row = lambda t: a[t][bass.ds(l, 1)]
                    sp.dma_start(wqkv[:], row("wqkv").rearrange("a p n -> (a p) n")).then_inc(q["attn_w_in"], 16)
                    sp.dma_start(wo[:], row("wo").rearrange("a (m r) n -> (a r) m n", r=P))\
                      .then_inc(q["attn_w_in"], 16)
                    sp.dma_start(scales[:], row("scales").broadcast_to([P, 4 * DH])).then_inc(q["attn_w_in"], 16)
                    sp.wait_ge(q["xa_ready"], l * NU + 1)
                    sp.dma_start(w1[:], row("w1").rearrange("a p n -> (a p) n")).then_inc(q["ff_w_in"], 16)
                    sp.dma_start(w2[:], row("w2").rearrange("a (k p) n -> (a p) k n", p=P)).then_inc(q["ff_w_in"], 16)
                    sp.dma_start(vecs[:], row("vecs").rearrange("a p n -> (a p) n")).then_inc(q["ff_w_in"], 16)
                sp.wait_ge(q["last"], 2)
                for b in range(2):
                    sp.dma_start(out[:, b, :], fs[:, b, :]).then_inc(q["out_done"], 16)
                sp.wait_ge(q["out_done"], 32)

            @block.gpsimd
            def _(pool):
                own = Link(pool, q["pool"])

                def hold():
                    pool.sem_inc(q["pool_turn"], 1)

                for name in "wo_mm tab xa_ready smax v_mm rotq rotk xb_ready pt_mm ssq k_t".split():
                    pool.sem_inc(q[name], 1)
                pool.wait_ge(q["tabs_in"], 48)
                with pool.Fori(0, DEPTH) as l:
                    pool.wait_ge(q["attn_w_in"], (l + 1) * 48)
                    pool.wait_ge(q["xa_ready"], l * NU + 1)
                    hold()

                    def body(cb, ca, t):
                        own.restart()
                        if cb is not None:
                            pool.wait_ge(q["smax"], 2 * cb + 1)
                            hold()
                            pool.tensor_copy(mask[:].unsqueeze(1), masks[:, bass.ds(t, 1), :]).then_inc(q["mask"], 1)
                        if ca is not None:
                            pool.wait_ge(q["v_mm"], 2 * ca + 1)
                            hold()
                            own(pool.tensor_copy(xs[0:64, :], xa[0:64, bass.ds((t + 1) * TILE + 1, HALO + TILE)]))
                            own(pool.tensor_copy(xs[64:128, :], xa[64:128, bass.ds((t + 1) * TILE, HALO + TILE)]))
                            own(pool.tensor_tensor(xs[64:128, HALO:HALO + 1], xs[64:128, HALO:HALO + 1],
                                                   cols[64:128, bass.ds(t + 1, 1)], ALU.mult))
                            own(pool.tensor_copy(xr[:, 0, 0:64], xs[:, 96:160]))
                            own(pool.tensor_copy(xr[:, 0, 64:128], xs[:, 32:96]))
                            own(pool.tensor_copy(xr[:, 1, 0:64], xs[:, 64:128]))
                            pool.tensor_copy(xr[:, 1, 64:128], xs[:, 0:64]).then_inc(q["xs"], 1)
                            pool.wait_ge(q["rotk"], ca + 1)
                            pool.tensor_tensor(tab[:].unsqueeze(1), tabs[:, bass.ds(t + 1, 1), :],
                                               scales[:].unsqueeze(1), ALU.mult).then_inc(q["tab"], 1)
                            pool.wait_ge(q["q_parts"], ca + 1)
                            hold()
                            pool.tensor_tensor(qr[:], qr[:], t2[:], ALU.add).then_inc(q["q_added"], 1)

                    tiles(pool, l * NT, body)

            @block.tensor
            def _(pe):
                def hold():
                    pe.sem_inc(q["pe_turn"], 1)

                def scores(cb):
                    pe.wait_ge(q["qk_in"], 2 * cb + 2)
                    hold()
                    for f in range(2):
                        for m in range(PAIRS):
                            for w in range(TILE // WIN):
                                e = (f + w // 2) % 2
                                ins = pe.matmul(ps[WIN * w:WIN * w + WIN, S0 + f, 64 * m:64 * m + 64],
                                                qt[64 * e:64 * e + 64, m, WIN * w:WIN * w + WIN],
                                                kt[64 * e:64 * e + 64, m, WIN * w:WIN * w + 2 * WIN],
                                                start=True, stop=True)
                        ins.then_inc(q["sim"], 1)

                def project_qk(ca):
                    pe.wait_ge(q["xs"], ca + 1)
                    for m in range(4):
                        ins = pe.matmul(ps[:, Q0 + m, :], xs[:, HALO:HALO + TILE], wqkv[:, 512 * m:512 * m + 512],
                                        start=True, stop=True)
                        if m % 2:
                            ins.then_inc(q["qk"], 1)

                def transpose_probs(cb):
                    pe.wait_ge(q["p_ready"], cb + 1)
                    for m in range(PAIRS):
                        ins = pe.transpose(ps[:, S0 + m // 4, TILE * (m % 4):TILE * (m % 4) + TILE],
                                           pr[:, m, :, :].rearrange("p f j -> p (f j)"), s.ident)
                        if m % 4 == 3:
                            ins.then_inc(q["pt_mm"], 1)

                def weigh_values(cb):
                    for m in range(PAIRS):
                        if m % 4 == 0:
                            pe.wait_ge(q["pt_in"], 2 * cb + m // 4 + 1)
                            hold()
                        for w in range(TILE // WIN):
                            for e in range(2):
                                f = (e + w // 2) % 2
                                v = 2 * (1 - w % 2) + e
                                o = 64 * m + WIN * (w % 2)
                                ins = pe.matmul(ps[64 * e:64 * e + 64, O0 + w // 2, o:o + WIN],
                                                vs[64 * f:64 * f + 64, v, DH * m:DH * m + DH],
                                                pt[64 * f:64 * f + 64, m, WIN * w:WIN * w + WIN],
                                                start=True, stop=True)
                    ins.then_inc(q["o_mm"], 1)

                def project_v(cb, ca):
                    wv = wqkv[:, 2 * INNER:3 * INNER].rearrange("p (m e d) -> p e m d", e=2, d=DH)
                    for r, (even, odd) in enumerate(((xs[:, HALO:HALO + TILE], xr[:, 0, :]),
                                                     (xs[:, 0:TILE], xr[:, 1, :]))):
                        if r and cb is not None:
                            pe.wait_ge(q["o_in"], cb + 1)
                        for e, x in enumerate((even, odd)):
                            ins = pe.matmul(ps[:, V0[r] + e, :].rearrange("p (m d) -> p m d", d=DH), x, wv[:, e],
                                            start=True, stop=True)
                        ins.then_inc(q["v_mm"], 1)

                def transpose_qk(ca):
                    for n, (src, bank0, ready, done) in enumerate(((qr, S0, q["rotq"], q["q_t"]),
                                                                   (kr, O0, q["rotk"], q["k_t"]))):
                        pe.wait_ge(ready, ca + 2)
                        pe.wait_ge(q["v_in"], 2 * ca + n + 1)
                        for m in range(PAIRS):
                            ins = pe.transpose(ps[:, bank0 + m // 4, TILE * (m % 4):TILE * (m % 4) + TILE],
                                               src[:, P * m:P * m + P], s.ident)
                        ins.then_inc(done, 1)

                def body(cb, ca, t):
                    if cb is not None:
                        scores(cb)
                    if ca is not None:
                        pe.wait_ge(q["xb_ready"], (ca if cb is None else cb) + 1)
                        project_qk(ca)
                    if cb is not None:
                        transpose_probs(cb)
                        weigh_values(cb)
                    if ca is not None:
                        project_v(cb, ca)
                    if ca is not None:
                        transpose_qk(ca)
                    if cb is not None:
                        pe.wait_ge(q["o_in"], cb + 1)
                        for m in range(PAIRS):
                            ins = pe.matmul(ps[:, Q0, 0:TILE], wo[:, m, :], ot[:, m, :], start=(m == 0),
                                            stop=(m == PAIRS - 1))
                        ins.then_inc(q["wo_mm"], 1)

                pe.wait_ge(q["cleared"], 1)
                with pe.Fori(0, DEPTH) as l:
                    pe.wait_ge(q["attn_w_in"], (l + 1) * 48)
                    tiles(pe, l * NT, body)
                    pe.wait_ge(q["xb_ready"], (l + 1) * NT + 1)
                    for n, (ready, src) in enumerate(((q["fs_ready"], fs), (q["squares2"], fq))):
                        for b in range(2):
                            pe.wait_ge(ready, 2 * l + b + 1)
                            for k in range(NB):
                                ins = pe.matmul(ps[:, 4 * b + k, 0:BL], s.ones[:], src[:, b, BL * k:BL * k + BL],
                                                start=True, stop=True)
                            ins.then_inc(q["ln_sums"], 1)
                    pe.wait_ge(q["ff_w_in"], (l + 1) * 48)
                    pe.wait_ge(q["xn_ready"], 2 * l + 2)
                    for k in range(NS + 2):
                        if k < NS:
                            (u, j), m = divmod(k, NCH), CH[k % NCH]
                            b, n = divmod(u, NB)
                            if k >= 3:
                                pe.wait_ge(q["hid_ready"], l * NS + k - 2)
                            for g in range(2):
                                ins = pe.matmul(ps[0:m, 2 * (k % 3) + g, 0:BL], w1[:, FI * g + P * j:FI * g + P * j + m],
                                                fs[:, b, BL * n:BL * n + BL], start=True, stop=True)
                            ins.then_inc(q["w1_mm"], 1)
                        if k >= 2:
                            r = k - 2
                            (u, j), m = divmod(r, NCH), CH[r % NCH]
                            if j == 0 and u >= 2:
                                pe.wait_ge(q["xa_ready"], l * NU + u)
                            pe.wait_ge(q["hid_ready"], l * NS + r + 1)
                            pe.matmul(ps[:, 6 + u % 2, 0:BL], w2[0:m, j, :], hid[0:m, r % 3, :], start=(j == 0),
                                      stop=(j == NCH - 1)).then_inc(q["w2_mm"], 1)

            @block.scalar
            def _(act):
                own = Link(act, q["act"])

                def body(cb, ca, t):
                    own.restart()
                    if cb is not None:
                        act.wait_ge(q["pt_mm"], 2 * cb + 1)
                        for f in range(2):
                            act.wait_ge(q["smax"], 2 * cb + f + 2)
                            act.activation(pr[:, :, f, :], s1[:, f, :, :], ACT.Exp, scale=DH ** 0.5)\
                               .then_inc(q["exp"], 1)
                    if ca is not None:
                        act.wait_ge(q["ssq"], ca + 1)
                        for n in range(2):
                            act.wait_ge(q["qk"], 2 * ca + n + 1)
                            act.activation(sq[:, INNER * n:INNER * n + INNER],
                                           two(Q0 + 2 * n).rearrange("p a n -> p (a n)"), ACT.Square)\
                               .then_inc(q["squares"], 1)
                    if cb is not None:
                        for k in range(2):
                            act.wait_ge(q["pt_mm"], 2 * cb + k + 2)
                            act.activation(pt[:, 4 * k:4 * k + 4, :].rearrange("p m t -> p (m t)"),
                                           ps[:, S0 + k, :], ACT.Copy).then_inc(q["pt_in"], 1)
                    if ca is not None:
                        act.wait_ge(q["ssq"], ca + 2)
                        own(act.activation(rn[:], rn[:], ACT.Ln, scale=2.0 ** 20))
                        own(act.activation(rn[:], rn[:], ACT.Exp, scale=-0.5))
                        act.activation(rn[:], rn[:], ACT.Copy, scale=2.0 ** 10).then_inc(q["rnorm"], 1)
                    if cb is not None:
                        act.wait_ge(q["o_mm"], cb + 1)
                        for w in range(2):
                            ins = act.activation(ot[:, :, 64 * w:64 * w + 64],
                                                 ps[:, O0 + w, :].rearrange("p (m t) -> p m t", t=64), ACT.Copy)
                            if w == 0:
                                own(ins)
                        ins.then_inc(q["o_in"], 1)
                    if ca is not None:
                        for r in range(2):
                            act.wait_ge(q["v_mm"], 2 * ca + r + 2)
                            act.activation(vs[:, 2 * r:2 * r + 2, :], two(V0[r]), ACT.Copy).then_inc(q["v_in"], 1)
                        act.wait_ge(q["q_t"], ca + 1)
                        act.activation(qt[:].rearrange("p (a m) t -> p a (m t)", a=2), two(S0), ACT.Copy)\
                           .then_inc(q["qk_in"], 1)
                        own(act.activation(kt[:, :, 0:HALO], kt[:, :, TILE:TILE + HALO], ACT.Copy,
                                           scale=cols[:, NT:NT + 1]))
                        act.wait_ge(q["k_t"], ca + 2)
                        for k in range(2):
                            ins = act.activation(kt[:, 4 * k:4 * k + 4, HALO:HALO + TILE],
                                                 ps[:, O0 + k, :].rearrange("p (m t) -> p m t", t=TILE), ACT.Copy)
                            if k == 0:
                                own(ins)
                        ins.then_inc(q["qk_in"], 1)
                        act.wait_ge(q["qk_in"], 2 * ca + 2)

                act.wait_ge(q["cleared"], 1)
                act.wait_ge(q["tabs_in"], 48)
                with act.Fori(0, DEPTH) as l:
                    act.preload_act_table_set(LN_EXP)
                    tiles(act, l * NT, body)
                    own.restart()
                    for b in range(2):
                        act.wait_ge(q["centered"], 2 * l + b + 1)
                        act.activation(fq[:, b, :], fs[:, b, :], ACT.Square).then_inc(q["squares2"], 1)
                    for b in range(2):
                        act.wait_ge(q["ln_sums"], 4 * l + b + 3)
                        own(act.activation(blk(fq, b), banks[b], ACT.Ln, scale=1.0 / D, bias=1e-5))
                        act.activation(fq[:, b, :], fq[:, b, :], ACT.Exp, scale=-0.5).then_inc(q["rstd"], 1)
                    act.wait_ge(q["ff_w_in"], (l + 1) * 48)
                    for k in range(NS):
                        j, m = k % NCH, CH[k % NCH]
                        act.wait_ge(q["w1_mm"], l * NS + k + 1)
                        act.activation(gel[0:m, k % 3, :], ps[0:m, 2 * (k % 3) + 1, 0:BL], ACT.Gelu,
                                       bias=vecs[0:m, 6 + j:7 + j]).then_inc(q["gelu"], 1)

            @block.vector
            def _(dve):
                own = Link(dve, q["dve"])

                def products(src0, dst, dst2, table):
                    src = heads(two(src0).rearrange("p a n -> p (a n)"))
                    tb = lambda lo, n: tab[:, table + lo:table + lo + n].unsqueeze(1).broadcast_to([P, HEADS, n])
                    own(dve.tensor_tensor(heads(dst[:]), src, tb(0, DH), ALU.mult))
                    own(dve.tensor_tensor(heads(dst2)[:, :, 0:32], src[:, :, 32:64], tb(DH, 32), ALU.mult))
                    return dve.tensor_tensor(heads(dst2)[:, :, 32:64], src[:, :, 0:32], tb(DH + 32, 32), ALU.mult)

                def normed(dst, norm):
                    return dve.tensor_tensor(heads(dst[:]), heads(dst[:]),
                                             rn[:, norm:norm + HEADS].unsqueeze(2).broadcast_to([P, HEADS, DH]),
                                             ALU.mult)

                def body(cb, ca, t):
                    own.restart()
                    if cb is not None:
                        dve.wait_ge(q["mask"], cb + 1)
                        for f in range(2):
                            dve.wait_ge(q["sim"], 2 * cb + f + 1)
                            sim = ps[:, S0 + f, :].rearrange("p (m j) -> p m j", j=64)
                            own(dve.tensor_tensor(s1[:, f], sim, mask[:].unsqueeze(1).broadcast_to([P, PAIRS, 64]),
                                                  ALU.add))
                            own(dve.tensor_reduce(mx[:, f, :], s1[:, f], AX_X, ALU.max))
                            dve.tensor_tensor(s1[:, f], s1[:, f],
                                              mx[:, f, :].unsqueeze(2).broadcast_to([P, PAIRS, 64]), ALU.subtract)\
                               .then_inc(q["smax"], 1)
                    if cb is not None:
                        dve.wait_ge(q["exp"], 2 * cb + 2)
                        prh = pr[:].rearrange("p m f j -> p (m f) j")
                        own(dve.tensor_reduce(rs[:], prh, AX_X, ALU.add))
                        own(dve.reciprocal(rs[:], rs[:]))
                        dve.tensor_tensor(prh, prh, rs[:].unsqueeze(2).broadcast_to([P, 2 * PAIRS, 64]), ALU.mult)\
                           .then_inc(q["p_ready"], 1)
                    if ca is not None:
                        dve.wait_ge(q["squares"], 2 * ca + 2)
                        dve.wait_ge(q["rotk"], ca + 1)
                        own(dve.tensor_reduce(rn[:], heads(sq), AX_X, ALU.add))
                        dve.tensor_scalar(rn[:], rn[:], 1e-24, None, ALU.max).then_inc(q["ssq"], 1)
                    if ca is not None:
                        dve.wait_ge(q["tab"], ca + 2)
                        dve.wait_ge(q["k_t"], ca + 1)
                        products(Q0, qr, t2[:], 0).then_inc(q["q_parts"], 1)
                        own(products(K0, kr, t3, 2 * DH))
                        own(dve.tensor_tensor(kr[:], kr[:], t3, ALU.add))
                        dve.wait_ge(q["rnorm"], ca + 1)
                        dve.wait_ge(q["q_added"], ca + 1)
                        normed(qr, 0).then_inc(q["rotq"], 1)
                        normed(kr, HEADS).then_inc(q["rotk"], 1)
                    if cb is not None:
                        x0 = t * TILE + XPAD
                        dve.wait_ge(q["wo_mm"], cb + 2)
                        dve.tensor_tensor(xb[:, bass.ds(x0, TILE)], xa[:, bass.ds(x0, TILE)], ps[:, Q0, 0:TILE],
                                          ALU.add).then_inc(q["xb_ready"], 1)

                own(dve.memset(xb[:, 0:XPAD], 0.0))
                dve.memset(kt[:], 0.0).then_inc(q["cleared"], 1)
                with dve.Fori(0, DEPTH) as l:
                    tiles(dve, l * NT, body)
                    dve.wait_ge(q["xb_ready"], (l + 1) * NT + 1)
                    dve.sem_inc(q["dve_turn"], 1)
                    own.restart()
                    for b in range(2):
                        x0 = XPAD + T * b
                        own(dve.tensor_copy(fs[0:64, b, :], xb[0:64, x0:x0 + T]))
                        own(dve.memset(fs[64:128, b, 0:1], 0.0))
                        dve.tensor_copy(fs[64:128, b, 1:T], xb[64:128, x0:x0 + T - 1]).then_inc(q["fs_ready"], 1)
                    dve.wait_ge(q["ff_w_in"], (l + 1) * 48)
                    for b in range(2):
                        dve.wait_ge(q["ln_sums"], 4 * l + b + 1)
                        dve.scalar_tensor_tensor(out=blk(fs, b), in0=banks[b], scalar=-1.0 / D, in1=blk(fs, b),
                                                 op0=ALU.mult, op1=ALU.add).then_inc(q["centered"], 1)
                    for b in range(2):
                        dve.wait_ge(q["rstd"], 2 * l + b + 1)
                        own(dve.tensor_tensor(fs[:, b, :], fs[:, b, :], fq[:, b, :], ALU.mult))
                        dve.tensor_scalar(fs[:, b, :], fs[:, b, :], vecs[:, 0:1], vecs[:, 1:2], ALU.mult, ALU.add)\
                           .then_inc(q["xn_ready"], 1)
                    for k in range(NS + 2):
                        if k < NS:
                            j, m = k % NCH, CH[k % NCH]
                            if k >= 3:
                                dve.wait_ge(q["w2_mm"], l * NS + k - 2)
                            dve.wait_ge(q["gelu"], l * NS + k + 1)
                            dve.scalar_tensor_tensor(out=hid[0:m, k % 3, :], in0=ps[0:m, 2 * (k % 3), 0:BL],
                                                     scalar=vecs[0:m, 3 + j:4 + j], in1=gel[0:m, k % 3, :],
                                                     op0=ALU.add, op1=ALU.mult).then_inc(q["hid_ready"], 1)
                        u, j = divmod(k - 2, NCH)
                        if j == NCH - 1 and u >= 0:
                            x0 = XPAD + BL * u
                            dve.wait_ge(q["w2_mm"], l * NS + k - 1)
                            dve.scalar_tensor_tensor(out=xa[:, x0:x0 + BL], in0=ps[:, 6 + u % 2, 0:BL],
                                                     scalar=vecs[:, 2:3], in1=xb[:, x0:x0 + BL],
                                                     op0=ALU.add, op1=ALU.add).then_inc(q["xa_ready"], 1)
                    dve.wait_ge(q["xa_ready"], (l + 1) * NU + 1)
                for b in range(2):
                    x0 = XPAD + T * b
                    dve.scalar_tensor_tensor(out=fs[:, b, :], in0=xa[:, x0:x0 + T], scalar=mod[:, GATE_B, b:b + 1],
                                             in1=s.x[:, b, :], op0=ALU.mult, op1=ALU.add).then_inc(q["last"], 1)



INPUTS = """L0_attn_x L0_attn_norm_in_w L0_attn_conv_w L0_attn_conv_b L0_attn_Wq L0_attn_Wk L0_attn_Wv L0_attn_Wo
L0_attn_Wspike L0_attn_Wau L0_attn_bau L0_attn_Wad L0_attn_bad L0_attn_alpha_spike L0_attn_Wbeta L0_attn_bbeta
L0_attn_beta_spike L0_attn_head_norm_w L0_attn_Wu1 L0_attn_bu1 L0_attn_Wu2 L0_attn_bu2 L0_attn_ff_norm_w
L0_attn_Wff1 L0_attn_Wff3 L0_attn_Wff2 L0_c L0_wmod""".split()


TRANSPOSED = {"L0_attn_x": (2, 0, 1), "L0_c": (1, 0)}
BY_PAIRS = ("L0_attn_beta_spike", "L0_attn_alpha_spike", "L0_attn_head_norm_w")


def laid_out(name, x):
    if name in BY_PAIRS:
        x = np.asarray(x).reshape(H // 2, 2, DK)
        return np.ascontiguousarray(x.transpose(1, 2, 0).reshape(2 * DK, H // 2))
    if name == "L0_attn_bbeta":
        return np.ascontiguousarray(np.asarray(x).reshape(H // 2, 2).T)
    return np.ascontiguousarray(np.transpose(x, TRANSPOSED[name]) if name in TRANSPOSED else x)


def layer_arrays(x):
    def columns(v):
        n = -(-v.shape[1] // P)
        out = np.zeros((v.shape[0], n * P), v.dtype)
        out[:, :v.shape[1]] = v
        return out.reshape(v.shape[0], n, P).transpose(0, 2, 1)

    half, inner = DH // 2, x["L0_ffn_b1"].shape[1] // 2
    w2 = x["L0_ffn_W2"]
    padded = np.zeros((w2.shape[0], -(-inner // P) * P, w2.shape[2]), w2.dtype)
    padded[:, :inner] = w2
    swapped = [np.concatenate([v, v[:, half:], v[:, :half]], axis=1)
               for v in (x["L0_ffn_q_scale"], x["L0_ffn_k_scale"])]
    vecs = [columns(x["L0_ffn_" + n]) for n in ("ln_g", "ln_b", "b2")]
    vecs += [columns(v) for v in (x["L0_ffn_b1"][:, :inner], x["L0_ffn_b1"][:, inner:])]
    return {"wqkv": x["L0_ffn_Wqkv"], "wo": x["L0_ffn_Wo"], "w1": x["L0_ffn_W1"], "w2": padded,
            "scales": np.concatenate(swapped, axis=1), "vecs": np.concatenate(vecs, axis=2)}


def kernel(**inputs):
    import concourse.bacc as bacc
    from concourse.bass_utils import run_bass_kernel_spmd

    nc = bacc.Bacc("TRN2", target_bir_lowering=False, num_devices=1)
    arrays, a, const = {}, {}, {}
    given = {name: laid_out(name, inputs[name]) for name in INPUTS}
    given |= layer_arrays({k: np.asarray(v) for k, v in inputs.items()})
    for name, x in given.items():
        arrays[f"in_{name}"] = x = np.ascontiguousarray(x)
        a[name] = nc.dram_tensor(f"in_{name}", x.shape, mybir.dt.from_np(x.dtype), kind="ExternalInput").ap()
    B, T, _ = inputs["L0_attn_x"].shape
    for name, x in shape_constants(T).items():
        arrays[f"const_{name}"] = x
        const[name] = nc.dram_tensor(f"const_{name}", x.shape, F32, kind="ExternalInput").ap()
    out = nc.dram_tensor("out", (D, B, T), F32, kind="ExternalOutput").ap()
    adaln_block(nc, a, const, out)
    r = run_bass_kernel_spmd(nc, [arrays], core_ids=[0])
    return np.ascontiguousarray(np.transpose(r.results[0]["out"], (1, 2, 0)))
```
